# Optimizing a Trainium2 kernel written in Bass

```python
import numpy as np
import jax
import jax.numpy as jnp

def _softmax(x, axis=-1):
    return jax.nn.softmax(x, axis=axis)

def _gelu(x):
    return jax.nn.gelu(x, approximate=True)

def _silu(x):
    return jax.nn.silu(x)

def _sigmoid(x):
    return jax.nn.sigmoid(x)

def _layernorm(x, axis=-1, eps=1e-05):
    m = jnp.mean(x, axis=axis, keepdims=True)
    v = jnp.var(x, axis=axis, keepdims=True)
    return (x - m) / jnp.sqrt(v + eps)

def _scatter_add(tgt, idx, src, axis=0):
    return tgt.at[idx].add(src)

def _segment_sum(src, seg, n):
    return jax.ops.segment_sum(src, seg, n)
kernel_name = 'mk_early_fusion_d1_tok_img512_r4_aaa30b'

def setup_inputs(seed: int=0):
    np.random.seed(seed)
    _w = jnp.asarray

    def _rec_inputs():
        import jax
        import jax.numpy as jnp
        _rk = jax.random.key(seed)
        x = -0.00040386 + 0.999972 * jax.random.normal(jax.random.fold_in(_rk, 1), (2, 3, 224, 224), jnp.float32)
        txt = 0.00170467 + 0.700178 * jax.random.normal(jax.random.fold_in(_rk, 2), (2, 512, 128), jnp.float32)
        return (x, txt)
    x, txt = _rec_inputs()

    def _L0_tok_setup():
        import jax, jax.numpy as jnp
        import numpy as np
        PATCH = 4
        EMBED = 128

        def _extract_patches(x):
            B, C, H, Wd = x.shape
            p = PATCH
            x = x.reshape(B, C, H // p, p, Wd // p, p)
            x = x.transpose(0, 2, 4, 1, 3, 5)
            return x.reshape(B, H // p * (Wd // p), C * p * p)
        key = jax.random.key(seed)
        k1, k2, k3, k4 = jax.random.split(key, 4)
        x = jax.random.normal(k1, (64, 3, 64, 64), dtype=jnp.float32)
        W = jax.random.normal(k2, (EMBED, PATCH * PATCH * 3), dtype=jnp.float32) * 0.1
        b = jax.random.normal(k3, (EMBED,), dtype=jnp.float32) * 0.1
        cls = jax.random.normal(k4, (1, 1, EMBED), dtype=jnp.float32)
        return {'x': x, 'W': W, 'b': b, 'cls': cls}
    _L0_tok_all = _L0_tok_setup()
    _L0_tok_in = {k: v for k, v in _L0_tok_all.items() if k in ('W', 'b', 'cls')}
    del _L0_tok_all

    def _L0_attn_setup():
        import jax, jax.numpy as jnp
        import numpy as np
        B, T, D = (64, 128, 128)
        H = 256
        I = 128
        MASK_VALUE = 0.0

        def _lstm_layer(x, mask, W, U, b):
            Hd = U.shape[0]
            xz = jnp.einsum('btd,dk->btk', x, W) + b
            xz_t = jnp.transpose(xz, (1, 0, 2))
            mask_t = jnp.transpose(mask, (1, 0))

            def step(carry, inp):
                h, c = carry
                z_in, m = inp
                z = z_in + h @ U
                i, f, g, o = jnp.split(z, 4, axis=-1)
                i = jax.nn.sigmoid(i)
                f = jax.nn.sigmoid(f)
                g = jnp.tanh(g)
                o = jax.nn.sigmoid(o)
                c_new = f * c + i * g
                h_new = o * jnp.tanh(c_new)
                m2 = m[:, None]
                h = jnp.where(m2, h_new, h)
                c = jnp.where(m2, c_new, c)
                return ((h, c), h)
            h0 = jnp.zeros((x.shape[0], Hd), dtype=x.dtype)
            c0 = jnp.zeros((x.shape[0], Hd), dtype=x.dtype)
            (_, _), hs = jax.lax.scan(step, (h0, c0), (xz_t, mask_t))
            return jnp.transpose(hs, (1, 0, 2))
        key = jax.random.key(seed)
        ks = jax.random.split(key, 7)
        s = 0.05
        inputs = jax.random.normal(ks[0], (B, T, D), dtype=jnp.float32)
        W0 = jax.random.normal(ks[1], (D, 4 * H), dtype=jnp.float32) * s
        U0 = jax.random.normal(ks[2], (H, 4 * H), dtype=jnp.float32) * s
        b0 = jnp.zeros((4 * H,), dtype=jnp.float32)
        W1 = jax.random.normal(ks[3], (H, 4 * I), dtype=jnp.float32) * s
        U1 = jax.random.normal(ks[4], (I, 4 * I), dtype=jnp.float32) * s
        b1 = jnp.zeros((4 * I,), dtype=jnp.float32)
        return {'inputs': inputs, 'W0': W0, 'U0': U0, 'b0': b0, 'W1': W1, 'U1': U1, 'b1': b1}
    _L0_attn_all = _L0_attn_setup()
    _L0_attn_in = {k: v for k, v in _L0_attn_all.items() if k in ('W0', 'U0', 'b0', 'W1', 'U1', 'b1')}
    del _L0_attn_all

    def _L0_ffn_setup():
        import jax, jax.numpy as jnp
        import numpy as np
        B, T, D, H = (2, 256, 128, 512)
        G, E = (4, 8)
        GK, EK = (2, 2)
        EPS = 1e-05
        SCALE = 0.02

        def _layernorm(x, g, b):
            m = jnp.mean(x, axis=-1, keepdims=True)
            xc = x - m
            v = jnp.mean(xc * xc, axis=-1, keepdims=True)
            return xc * jax.lax.rsqrt(v + EPS) * g + b

        def _topk_gate(logits, k, n):
            v, i = jax.lax.top_k(logits, k)
            sc = jax.nn.softmax(v, axis=-1)
            return jnp.sum(jax.nn.one_hot(i, n, dtype=logits.dtype) * sc[..., None], axis=-2)
        key = jax.random.key(seed)
        ks = jax.random.split(key, 6)
        return {'inp': jax.random.normal(ks[0], (B, T, D), jnp.float32), 'ln_g': jnp.ones((D,), jnp.float32), 'ln_b': jnp.zeros((D,), jnp.float32), 'wg_group': jax.random.normal(ks[1], (D, G), jnp.float32) * SCALE, 'wg_inner': jax.random.normal(ks[2], (G, D, E), jnp.float32) * SCALE, 'W1': jax.random.normal(ks[3], (G, E, D, H), jnp.float32) * SCALE, 'b1': jnp.zeros((G, E, H), jnp.float32), 'W2': jax.random.normal(ks[4], (G, E, H, D), jnp.float32) * SCALE, 'b2': jnp.zeros((G, E, D), jnp.float32), 'gln_g': jnp.ones((G, D), jnp.float32), 'gln_b': jnp.zeros((G, D), jnp.float32)}
    _L0_ffn_all = _L0_ffn_setup()
    _L0_ffn_in = {k: v for k, v in _L0_ffn_all.items() if k in ('ln_g', 'ln_b', 'wg_group', 'wg_inner', 'W1', 'b1', 'W2', 'b2', 'gln_g', 'gln_b')}
    del _L0_ffn_all
    return {'x': x, 'txt': txt, 'L0_tok_W': _L0_tok_in['W'], 'L0_tok_b': _L0_tok_in['b'], 'L0_tok_cls': _L0_tok_in['cls'], 'L0_attn_W0': _L0_attn_in['W0'], 'L0_attn_U0': _L0_attn_in['U0'], 'L0_attn_b0': _L0_attn_in['b0'], 'L0_attn_W1': _L0_attn_in['W1'], 'L0_attn_U1': _L0_attn_in['U1'], 'L0_attn_b1': _L0_attn_in['b1'], 'L0_ffn_ln_g': _L0_ffn_in['ln_g'], 'L0_ffn_ln_b': _L0_ffn_in['ln_b'], 'L0_ffn_wg_group': _L0_ffn_in['wg_group'], 'L0_ffn_wg_inner': _L0_ffn_in['wg_inner'], 'L0_ffn_W1': _L0_ffn_in['W1'], 'L0_ffn_b1': _L0_ffn_in['b1'], 'L0_ffn_W2': _L0_ffn_in['W2'], 'L0_ffn_b2': _L0_ffn_in['b2'], 'L0_ffn_gln_g': _L0_ffn_in['gln_g'], 'L0_ffn_gln_b': _L0_ffn_in['gln_b']}

def reference(x, txt, L0_tok_W, L0_tok_b, L0_tok_cls, L0_attn_W0, L0_attn_U0, L0_attn_b0, L0_attn_W1, L0_attn_U1, L0_attn_b1, L0_ffn_ln_g, L0_ffn_ln_b, L0_ffn_wg_group, L0_ffn_wg_inner, L0_ffn_W1, L0_ffn_b1, L0_ffn_W2, L0_ffn_b2, L0_ffn_gln_g, L0_ffn_gln_b):
    import jax
    import jax.numpy as jnp

    def _L0_tok_ref(x, W, b, cls):
        import jax, jax.numpy as jnp
        import numpy as np
        PATCH = 4
        EMBED = 128

        def _extract_patches(x):
            B, C, H, Wd = x.shape
            p = PATCH
            x = x.reshape(B, C, H // p, p, Wd // p, p)
            x = x.transpose(0, 2, 4, 1, 3, 5)
            return x.reshape(B, H // p * (Wd // p), C * p * p)
        patches = _extract_patches(x)
        emb = jnp.einsum('blk,ek->ble', patches, W) + b
        B = x.shape[0]
        cls_tok = jnp.broadcast_to(cls, (B, 1, EMBED))
        return jnp.concatenate([cls_tok, emb], axis=1)

    def _L0_attn_ref(inputs, W0, U0, b0, W1, U1, b1):
        import jax, jax.numpy as jnp
        import numpy as np
        B, T, D = (64, 128, 128)
        H = 256
        I = 128
        MASK_VALUE = 0.0

        def _lstm_layer(x, mask, W, U, b):
            Hd = U.shape[0]
            xz = jnp.einsum('btd,dk->btk', x, W) + b
            xz_t = jnp.transpose(xz, (1, 0, 2))
            mask_t = jnp.transpose(mask, (1, 0))

            def step(carry, inp):
                h, c = carry
                z_in, m = inp
                z = z_in + h @ U
                i, f, g, o = jnp.split(z, 4, axis=-1)
                i = jax.nn.sigmoid(i)
                f = jax.nn.sigmoid(f)
                g = jnp.tanh(g)
                o = jax.nn.sigmoid(o)
                c_new = f * c + i * g
                h_new = o * jnp.tanh(c_new)
                m2 = m[:, None]
                h = jnp.where(m2, h_new, h)
                c = jnp.where(m2, c_new, c)
                return ((h, c), h)
            h0 = jnp.zeros((x.shape[0], Hd), dtype=x.dtype)
            c0 = jnp.zeros((x.shape[0], Hd), dtype=x.dtype)
            (_, _), hs = jax.lax.scan(step, (h0, c0), (xz_t, mask_t))
            return jnp.transpose(hs, (1, 0, 2))
        mask = jnp.any(inputs != MASK_VALUE, axis=-1)
        x = _lstm_layer(inputs, mask, W0, U0, b0)
        latent = _lstm_layer(x, mask, W1, U1, b1)
        return latent

    def _L0_ffn_ref(inp, ln_g, ln_b, wg_group, wg_inner, W1, b1, W2, b2, gln_g, gln_b):
        import jax, jax.numpy as jnp
        import numpy as np
        B, T, D, H = (2, 256, 128, 512)
        G, E = (4, 8)
        GK, EK = (2, 2)
        EPS = 1e-05
        SCALE = 0.02

        def _layernorm(x, g, b):
            m = jnp.mean(x, axis=-1, keepdims=True)
            xc = x - m
            v = jnp.mean(xc * xc, axis=-1, keepdims=True)
            return xc * jax.lax.rsqrt(v + EPS) * g + b

        def _topk_gate(logits, k, n):
            v, i = jax.lax.top_k(logits, k)
            sc = jax.nn.softmax(v, axis=-1)
            return jnp.sum(jax.nn.one_hot(i, n, dtype=logits.dtype) * sc[..., None], axis=-2)
        b, t, d = inp.shape
        x = inp.reshape(-1, d)
        gw = _topk_gate(x @ wg_group, GK, G)
        z = _layernorm(x, ln_g, ln_b)
        out = jnp.zeros_like(x)
        for g in range(G):
            iw = _topk_gate(z @ wg_inner[g], EK, E)
            moe = jnp.zeros_like(z)
            for e in range(E):
                h = jax.nn.relu(z @ W1[g, e] + b1[g, e])
                moe = moe + iw[:, e:e + 1] * (h @ W2[g, e] + b2[g, e])
            y = _layernorm(z + moe, gln_g[g], gln_b[g])
            out = out + gw[:, g:g + 1] * y
        return out.reshape(b, t, d) + inp
    h = _L0_tok_ref(x, L0_tok_W, L0_tok_b, L0_tok_cls)
    h = jnp.concatenate([h, txt], axis=1)
    h = h + _L0_attn_ref(_layernorm(h, axis=-1), L0_attn_W0, L0_attn_U0, L0_attn_b0, L0_attn_W1, L0_attn_U1, L0_attn_b1)
    h = h + _L0_ffn_ref(_layernorm(h, axis=-1), L0_ffn_ln_g, L0_ffn_ln_b, L0_ffn_wg_group, L0_ffn_wg_inner, L0_ffn_W1, L0_ffn_b1, L0_ffn_W2, L0_ffn_b2, L0_ffn_gln_g, L0_ffn_gln_b)
    return h

_drawn_inputs = setup_inputs


def setup_inputs(seed=0):
    import zlib

    import numpy as np

    out = dict(_drawn_inputs(seed))
    spreads = {'L0_attn_b0': (0.0, 0.304),
     'L0_attn_b1': (0.0, 0.1),
     'L0_ffn_ln_g': (1.0, 0.2),
     'L0_ffn_ln_b': (0.0, 0.1),
     'L0_ffn_b1': (0.0, 0.8),
     'L0_ffn_b2': (0.0, 0.435),
     'L0_ffn_gln_g': (1.0, 0.2),
     'L0_ffn_gln_b': (0.0, 0.281)}
    factors = {'L0_tok_cls': 3.018,
     'L0_attn_U0': 2.88,
     'L0_ffn_wg_inner': 2.712,
     'L0_ffn_W1': 4.858,
     'L0_ffn_W2': 3.756}
    for name, (base, spread) in spreads.items():
        noise = np.random.default_rng([zlib.crc32(name.encode()), seed]).standard_normal(out[name].shape)
        drawn = base * np.exp(spread * noise) if base else spread * noise
        out[name] = jnp.asarray(drawn.astype(out[name].dtype))
    for name, factor in factors.items():
        out[name] = (out[name] * factor).astype(out[name].dtype)
    return out
```

```python
from contextlib import ExitStack

import concourse.bass as bass
from concourse import mybir

ALU = mybir.AluOpType
ACT = mybir.ActivationFunctionType
F32 = mybir.dt.float32
F16 = mybir.dt.float16
BF16 = mybir.dt.bfloat16
U16 = mybir.dt.uint16
U32 = mybir.dt.uint32

P = 128
NB = 2
EPS = 1e-5
SAT = 32768.0
BODY = 64
HALF = BODY // 2
LAG = BODY - 1
NT = NB * BODY
GATES = (0, 1, 3, 2)
X, Y, Z = range(3)


TOKENS = 2


def done(n):
    return n + 1 + TOKENS


def freed(n):
    return n + 1


def make_tokens(nc, tokens, ident, XNT, CNT, RHS, x, txt, tok_W, tok_b, tok_cls, T, TP):
    C, IH, IW = x.shape[1:]
    PS = 4
    GI, GJ = IH // PS, IW // PS
    KP = C * PS * PS
    NR = NB * GI
    NTILE = TP // BODY
    assert GJ % 2 == 0 and NTILE % 2 == 0
    with ExitStack() as ctx:
        def sb(name, shape, dt=F32):
            return ctx.enter_context(nc.sbuf_tensor(name, shape, dt))

        def psum(name):
            return ctx.enter_context(nc.psum_tensor(name, [P, 512], F32))

        def sem(name):
            return ctx.enter_context(nc.semaphore(name))

        img = sb("img", [NR, C * PS, IW])
        wtok = sb("wtok", [P, KP])
        wtokT = sb("wtokT", [KP, P])
        btok = sb("btok", [NR, P])
        patch = sb("patch", [NR, 2, KP])
        patchT = sb("patchT", [KP, 2, NR])
        emb = sb("emb", [NR, 2, P])
        zrow = sb("zrow", [(TP - T) * NB, P])
        tile = sb("tile", [P, 2, P])
        xn = sb("xn", [P, 2, P])
        stats = sb("stats", [P, 2, 6])
        mv = sb("mv", [P, 2, 2])
        std = sb("std", [P, 2])
        rstd = sb("rstd", [P, 2])
        eps = sb("eps", [P, 1])
        ones = sb("ones", [P, P], BF16)
        live = sb("live", [P, 2, P], BF16)
        dead = sb("dead", [1, RHS.shape[1]])
        pT = [psum("pT0"), psum("pT1")]
        pE = [psum("pE0"), psum("pE1")]
        pX = [psum("pX0"), psum("pX1")]
        pC = [psum("pC0"), psum("pC1")]

        inputs_in = sem("inputs_in")
        consts_done = sem("consts_done")
        ident_done = sem("ident_done")
        pads_done = sem("pads_done")
        rest_out = sem("rest_out")
        patch_cut = sem("patch_cut")
        patch_turned = sem("patch_turned")
        patchT_done = sem("patchT_done")
        emb_made = sem("emb_made")
        emb_done = sem("emb_done")
        emb_out = [sem("emb_out0"), sem("emb_out1")]
        wtok_turned = sem("wtok_turned")
        wtokT_done = sem("wtokT_done")
        tile_in = [sem("tile_in0"), sem("tile_in1")]
        stats_done = sem("stats_done")
        mv_done = sem("mv_done")
        std_done = sem("std_done")
        rstd_done = sem("rstd_done")
        xn_done = sem("xn_done")
        xn_turned = sem("xn_turned")
        xnt_done = sem("xnt_done")
        live_done = sem("live_done")
        counted = sem("counted")
        dead_done = sem("dead_done")
        dead_out = sem("dead_out")
        block = ctx.enter_context(nc.Block())

        emb_rows = tokens[1:1 + GI * GJ, :, :].rearrange("(i j) b d -> b i j d", j=GJ)
        tiles = tokens.rearrange("(n t) b d -> n (t b) d", t=BODY)

        @block.sync
        def _(sp):
            for b in range(NB):
                for c in range(C):
                    sp.dma_start(img[b * GI:(b + 1) * GI, c * PS:(c + 1) * PS, :],
                                 x[b, c].rearrange("(i p) w -> i p w", p=PS)).then_inc(inputs_in, 16)
            sp.dma_start(wtok[:, :], tok_W).then_inc(inputs_in, 16)
            sp.dma_start(btok[:, :], tok_b.rearrange("(a d) -> a d", a=1).to_broadcast([NR, P]))\
                .then_inc(inputs_in, 16)
            for b in range(NB):
                sp.dma_start(tokens[1 + GI * GJ:T, b, :], txt[b]).then_inc(rest_out, 16)
                sp.dma_start(tokens[0:1, b, :], tok_cls[0]).then_inc(rest_out, 16)
            sp.wait_ge(consts_done, 3)
            sp.dma_start(tokens[T:TP].rearrange("t b d -> (t b) d"), zrow[:, :]).then_inc(rest_out, 16)
            with sp.Fori(0, GJ // 2) as pair:
                j = 2 * pair
                for u in range(2):
                    sp.wait_ge(emb_done, done(j + u))
                    for b in range(NB):
                        sp.dma_start(emb_rows[b, :, bass.ds(j + u, 1), :].rearrange("i a d -> i (a d)"),
                                     emb[b * GI:(b + 1) * GI, u, :]).then_inc(emb_out[u], 16)
            sp.wait_ge(rest_out, 16 * (2 * NB + 1))
            for u in range(2):
                sp.wait_ge(emb_out[u], 16 * NB * (GJ // 2 + 1))
            with sp.Fori(0, NTILE // 2) as pair:
                i = 2 * pair
                for u in range(2):
                    sp.wait_ge(xn_done, freed(i + u))
                    sp.dma_start(tile[:, u, :], tiles[bass.ds(i + u, 1)].rearrange("n p d -> (n p) d"))\
                        .then_inc(tile_in[u], 16)
            sp.wait_ge(dead_done, NTILE + TOKENS)
            sp.wait_ge(pads_done, 6)
            sp.dma_start(RHS[1:2, :], dead[:, :]).then_inc(dead_out, 16)
            sp.wait_ge(dead_out, 16)

        @block.gpsimd
        def _(pool):
            pool.memset(zrow[:, :], 0.0).then_inc(consts_done, 1)
            pool.memset(eps[:, :], EPS).then_inc(consts_done, 1)
            pool.memset(ones[:, :], 1.0).then_inc(consts_done, 1)
            pool.memset(ident[:, :], 0.0).then_inc(ident_done, 1)
            pool.wait_ge(ident_done, 1)
            pool.affine_select(out=ident[:, :], in_=ident[:, :], compare_op=ALU.not_equal, fill=1.0, base=0,
                               pattern=[[-1, P]], channel_multiplier=1).then_inc(ident_done, 1)
            pool.memset(CNT[:, 0:LAG * NB], 0.0).then_inc(pads_done, 1)
            pool.memset(CNT[:, (LAG + TP) * NB:], 0.0).then_inc(pads_done, 1)
            pool.memset(dead[:, 0:LAG * NB], 1.0).then_inc(pads_done, 1)
            pool.memset(dead[:, (LAG + TP) * NB:], 1.0).then_inc(pads_done, 1)
            pool.memset(XNT[:, TP * NB:], 0.0).then_inc(pads_done, 1)
            pool.memset(RHS[0:1, :], 1.0).then_inc(pads_done, 1)

        @block.tensor
        def _(pe):
            pe.sem_inc(patch_turned, TOKENS)
            pe.sem_inc(emb_made, TOKENS)
            pe.sem_inc(xn_turned, TOKENS)
            pe.sem_inc(counted, TOKENS)
            pe.wait_ge(ident_done, 2)
            pe.wait_ge(inputs_in, 16 * (NB * C + 2))
            pe.transpose(pE[0][0:KP, 0:P], wtok[:, :], ident[:, :]).then_inc(wtok_turned, 1)
            pe.wait_ge(wtokT_done, 1)
            with pe.Fori(0, GJ // 2) as pair:
                j = 2 * pair
                for u in range(2):
                    pe.wait_ge(patch_cut, j + u + 1)
                    pe.wait_ge(patchT_done, freed(j + u))
                    pe.matmul(pT[u][0:KP, 0:NR], patch[:, u, :], ident[0:NR, 0:NR], start=True, stop=True)\
                        .then_inc(patch_turned, 1)
                for u in range(2):
                    pe.wait_ge(patchT_done, done(j + u))
                    pe.wait_ge(emb_done, freed(j + u))
                    pe.matmul(pE[u][0:NR, 0:P], patchT[:, u, :], wtokT[:, :], start=True, stop=True)\
                        .then_inc(emb_made, 1)
            with pe.Fori(0, NTILE // 2) as pair:
                i = 2 * pair
                for u in range(2):
                    pe.wait_ge(xn_done, done(i + u))
                    pe.wait_ge(xnt_done, freed(i + u))
                    pe.transpose(pX[u][:, 0:P], xn[:, u, :], ident[:, :]).then_inc(xn_turned, 1)
                for u in range(2):
                    pe.wait_ge(live_done, i + u + 1)
                    pe.wait_ge(dead_done, freed(i + u))
                    pe.matmul(pC[u][:, 0:P], ones[:, :], live[:, u, :], start=True, stop=True).then_inc(counted, 1)

        @block.scalar
        def _(act):
            act.sem_inc(patchT_done, TOKENS)
            act.sem_inc(xnt_done, TOKENS)
            act.wait_ge(wtok_turned, 1)
            nc.scalar.copy(wtokT[:, :], pE[0][0:KP, 0:P]).then_inc(wtokT_done, 1)
            with act.Fori(0, GJ // 2) as pair:
                j = 2 * pair
                for u in range(2):
                    act.wait_ge(patch_turned, done(j + u))
                    act.wait_ge(emb_made, freed(j + u))
                    nc.scalar.copy(patchT[:, u, :], pT[u][0:KP, 0:NR]).then_inc(patchT_done, 1)
            act.wait_ge(consts_done, 3)
            with act.Fori(0, NTILE // 2) as pair:
                i = 2 * pair
                for u in range(2):
                    act.wait_ge(mv_done, i + u + 1)
                    nc.scalar.activation(std[:, u:u + 1], mv[:, u, 1:2], ACT.Sqrt, bias=eps[:, :])\
                        .then_inc(std_done, 1)
                for u in range(2):
                    act.wait_ge(xn_turned, done(i + u))
                    nc.scalar.copy(XNT[:, bass.ds((i + u) * NT, NT)], pX[u][:, 0:P]).then_inc(xnt_done, 1)

        @block.vector
        def _(dve):
            dve.sem_inc(emb_done, TOKENS)
            dve.sem_inc(xn_done, TOKENS)
            dve.sem_inc(dead_done, TOKENS)
            for u in range(2):
                dve.sem_inc(emb_out[u], NB * 16)
            dve.wait_ge(inputs_in, 16 * (NB * C + 2))
            with dve.Fori(0, GJ // 2) as pair:
                j = 2 * pair
                for u in range(2):
                    dve.wait_ge(patch_turned, freed(j + u))
                    nc.vector.tensor_copy(patch[:, u, :].rearrange("p (r w) -> p r w", w=PS),
                                          img[:, :, bass.ds((j + u) * PS, PS)]).then_inc(patch_cut, 1)
                for u in range(2):
                    dve.wait_ge(emb_made, done(j + u))
                    dve.wait_ge(emb_out[u], NB * 16 * (pair + 1))
                    nc.vector.tensor_tensor(emb[:, u, :], pE[u][0:NR, 0:P], btok[:, :], ALU.add)\
                        .then_inc(emb_done, 1)
            dve.wait_ge(consts_done, 3)
            with dve.Fori(0, NTILE // 2) as pair:
                i = 2 * pair
                for u in range(2):
                    dve.wait_ge(tile_in[u], 8 * i + 16)
                    nc.vector.bn_stats(stats[:, u, :], tile[:, u, :]).then_inc(stats_done, 1)
                for u in range(2):
                    dve.wait_ge(stats_done, i + u + 1)
                    nc.vector.memset(rstd[:, u:u + 1], 0.0)
                    nc.vector.bn_aggr(mv[:, u, :], stats[:, u, :]).then_inc(mv_done, 1)
                for u in range(2):
                    dve.wait_ge(std_done, i + u + 1)
                    nc.vector.reciprocal(rstd[:, u:u + 1], std[:, u:u + 1]).then_inc(rstd_done, 1)
                for u in range(2):
                    dve.wait_ge(rstd_done, i + u + 1)
                    dve.wait_ge(xn_turned, freed(i + u))
                    nc.vector.tensor_scalar(xn[:, u, :], tile[:, u, :], mv[:, u, 0:1], rstd[:, u:u + 1],
                                            ALU.subtract, ALU.mult).then_inc(xn_done, 1)
                for u in range(2):
                    dve.wait_ge(xnt_done, done(i + u))
                    dve.wait_ge(counted, freed(i + u))
                    nc.vector.tensor_scalar(live[:, u, :], XNT[:, bass.ds((i + u) * NT, NT)], 0.0, None,
                                            ALU.not_equal).then_inc(live_done, 1)
                for u in range(2):
                    dve.wait_ge(counted, done(i + u))
                    nc.vector.tensor_copy(CNT[:, bass.ds((i + u) * NT + LAG * NB, NT)], pC[u][:, 0:P])
                    nc.vector.tensor_scalar(dead[:, bass.ds((i + u) * NT + LAG * NB, NT)], pC[u][0:1, 0:P], 0.0, None,
                                            ALU.is_equal).then_inc(dead_done, 1)


def recur(nc, XNT, CNT, RHS, LAT, W0, U0, b0, W1, U1, b1, NBODY):
    H0, H1 = U0.shape[0], U1.shape[0]
    assert H0 == 2 * P and H1 == P
    with ExitStack() as ctx:
        def sb(name, shape, dt=F32):
            return ctx.enter_context(nc.sbuf_tensor(name, shape, dt))

        def sem(name):
            return ctx.enter_context(nc.semaphore(name))

        def each(make, name):
            return [make(f"{name}{c}") for c in "XYZ"]

        w0 = sb("w0", [P, 4 * H0])
        w1 = sb("w1", [P, 2, 4 * H1])
        u0f = sb("u0f", [P, 2, 4 * H0])
        u1f = sb("u1f", [P, 4 * H1])
        u0 = sb("u0", [P, 2, 2, 4 * H0], F16)
        u1 = sb("u1", [P, 2, 4 * H1], F16)
        bw = sb("bw", [2, 4 * (H0 + H1)])
        satrow = sb("satrow", [1, 4 * (H0 + H1)])
        h = each(lambda n: sb(n, [P, 2, 2, NB], F16), "h")
        sg = each(lambda n: sb(n, [P, 3 * NB]), "sg")
        gc = each(lambda n: sb(n, [P, 2 * NB]), "gc")
        pr = each(lambda n: sb(n, [P, 2 * NB]), "pr")
        og = each(lambda n: sb(n, [P, NB]), "og")
        tc = each(lambda n: sb(n, [P, NB]), "tc")
        hist = sb("hist", [P, 3, BODY, NB])
        mask = sb("mask", [P, 2, BODY, NB], U16)
        pz = [[ctx.enter_context(nc.psum_tensor(f"z{c}{p}", [P, HALF, 4, NB], F32)) for p in range(2)] for c in "XYZ"]

        weights_in = sem("weights_in")
        sat_done = sem("sat_done")
        sat_in = sem("sat_in")
        split_done = sem("split_done")
        state_zero = sem("state_zero")
        z_ready = each(sem, "z_ready")
        gates_ready = each(sem, "gates_ready")
        products_ready = each(sem, "products_ready")
        cell_ready = each(sem, "cell_ready")
        tanh_ready = each(sem, "tanh_ready")
        high_ready = each(sem, "high_ready")
        full_ready = each(sem, "full_ready")
        low_ready = each(sem, "low_ready")
        mask_ready = sem("mask_ready")
        lat_copied = sem("lat_copied")
        block = ctx.enter_context(nc.Block())

        @block.sync
        def _(sp):
            sp.dma_start(u0f[:, :, :], U0.rearrange("(k p) n -> p k n", p=P)).then_inc(weights_in, 16)
            sp.dma_start(u1f[:, :], U1).then_inc(weights_in, 16)
            sp.dma_start(w0[:, :], W0).then_inc(weights_in, 16)
            sp.dma_start(w1[:, :, :], W1.rearrange("(k p) n -> p k n", p=P)).then_inc(weights_in, 16)
            sp.dma_start(bw[0:1, 0:4 * H0], b0.rearrange("(a n) -> a n", a=1)).then_inc(weights_in, 16)
            sp.dma_start(bw[0:1, 4 * H0:], b1.rearrange("(a n) -> a n", a=1)).then_inc(weights_in, 16)
            sp.wait_ge(sat_done, 5)
            sp.dma_start(bw[1:2, :], satrow[:, :]).then_inc(sat_in, 16)

        @block.gpsimd
        def _(pool):
            pool.memset(satrow[:, :], 0.0).then_inc(sat_done, 1)
            pool.wait_ge(sat_done, 1)
            for base, n in ((0, H0), (4 * H0, H1)):
                pool.memset(satrow[:, base:base + n], -SAT).then_inc(sat_done, 1)
                pool.memset(satrow[:, base + n:base + 2 * n], SAT).then_inc(sat_done, 1)

            def copy_masks(half, t0):
                nc.gpsimd.tensor_copy(mask[:, 0, half * HALF:(half + 1) * HALF, :].rearrange("p t b -> p (t b)"),
                                      CNT[:, bass.ds((t0 + LAG) * NB, HALF * NB)]).then_inc(mask_ready, 1)
                nc.gpsimd.tensor_copy(mask[:, 1, half * HALF:(half + 1) * HALF, :].rearrange("p t b -> p (t b)"),
                                      CNT[:, bass.ds(t0 * NB, HALF * NB)]).then_inc(mask_ready, 1)

            def copy_out(half, at):
                nc.gpsimd.tensor_copy(LAT[:, bass.ds(at * NB, HALF * NB)],
                                      hist[:, Z, half * HALF:(half + 1) * HALF, :].rearrange("p t b -> p (t b)"))\
                    .then_inc(lat_copied, 1)

            pool.sem_inc(lat_copied, 1)
            pool.memset(LAT[:, (NBODY * BODY + HALF) * NB:], 0.0)
            copy_masks(0, 0)
            with pool.Fori(0, NBODY) as i:
                s0 = i * BODY
                pool.wait_ge(low_ready[Z], s0 + 1)
                copy_masks(1, s0 + HALF)
                pool.wait_ge(low_ready[Z], s0 + 2)
                copy_out(1, s0)
                pool.wait_ge(low_ready[Z], s0 + HALF + 1)
                copy_masks(0, s0 + BODY)
                pool.wait_ge(low_ready[Z], s0 + HALF + 2)
                copy_out(0, s0 + HALF)
            pool.wait_ge(low_ready[Z], NBODY * BODY + 1)
            copy_out(1, NBODY * BODY)

        def projections(pe, half, t0):
            def bias(c, g, lhs, base, at):
                return lambda: pe.matmul(pz[c][half][:, :, g, :], bw[:, lhs:lhs + P],
                                         RHS[:, bass.ds((t0 + at) * NB, HALF * NB)],
                                         start=(g == 0), stop=False, skip_group_check=True)

            def from_tokens(c, g, lhs):
                return lambda: pe.matmul(pz[c][half][:, :, g, :], w0[:, lhs:lhs + P],
                                         XNT[:, bass.ds(t0 * NB, HALF * NB)],
                                         start=False, stop=False, skip_group_check=True)

            def from_layer0(g, k, lhs):
                return lambda: pe.matmul(pz[Z][half][:, :, g, :], w1[:, k, lhs:lhs + P],
                                         hist[:, k, half * HALF:(half + 1) * HALF, :].rearrange("p t b -> p (t b)"),
                                         start=False, stop=False, skip_group_check=True)

            work = []
            for c in (X, Y):
                for g, gate in enumerate(GATES):
                    col = gate * H0 + c * P
                    work += [bias(c, g, col, 0, LAG), from_tokens(c, g, col)]
            for g, gate in enumerate(GATES):
                col = gate * H1
                work += [bias(Z, g, 4 * H0 + col, 0, 0), from_layer0(g, 0, col), from_layer0(g, 1, col)]
            return work

        @block.tensor
        def _(pe):
            pe.wait_ge(weights_in, 16 * 6)
            pe.wait_ge(sat_in, 16)
            pe.wait_ge(split_done, 4)
            pe.wait_ge(state_zero, 1)
            for mm in projections(pe, 0, 0):
                mm()

            def product(out, weights, state, last=False):
                return pe.matmul(out, weights, state, start=False, stop=last, skip_group_check=True)

            def step(j, s):
                half, jj = j // HALF, j % HALF
                old = (j + 1) % 2
                hi = [h[c][:, old, 0, :] for c in (X, Y, Z)]
                lo = [h[c][:, old, 1, :] for c in (X, Y, Z)]

                def high(c, k, gates=range(4)):
                    for g in gates:
                        col = GATES[g] * H0 + c * P
                        for part in range(2):
                            mm = product(pz[c][half][:, jj, g, :], u0[:, part, k, col:col + P], hi[k])
                    return mm

                def low(c, k):
                    for g in range(4):
                        col = GATES[g] * H0 + c * P
                        mm = product(pz[c][half][:, jj, g, :], u0[:, 0, k, col:col + P], lo[k], last=(k == Y))
                    return mm

                pe.wait_ge(high_ready[X], s + 1)
                high(X, X)
                high(Y, X, range(2))
                pe.wait_ge(low_ready[X], s + 1)
                low(X, X)
                pe.wait_ge(high_ready[Y], s + 1)
                high(X, Y)
                pe.wait_ge(low_ready[Y], s + 1)
                low(X, Y).then_inc(z_ready[X], 1)
                high(Y, X, range(2, 4))
                low(Y, X)
                high(Y, Y)
                low(Y, Y).then_inc(z_ready[Y], 1)
                pe.wait_ge(high_ready[Z], s + 1)
                for g, gate in enumerate(GATES):
                    for part in range(2):
                        product(pz[Z][half][:, jj, g, :], u1[:, part, gate * H1:(gate + 1) * H1], hi[Z])
                pe.wait_ge(low_ready[Z], s + 1)
                for g, gate in enumerate(GATES):
                    mm = product(pz[Z][half][:, jj, g, :], u1[:, 0, gate * H1:(gate + 1) * H1], lo[Z], last=True)
                mm.then_inc(z_ready[Z], 1)

            with pe.Fori(0, NBODY) as i:
                s0 = i * BODY
                for half in range(2):
                    work = projections(pe, 1 - half, s0 + (half + 1) * HALF)
                    for jj in range(HALF):
                        step(half * HALF + jj, s0 + half * HALF + jj)
                        if jj >= 1 and work:
                            work.pop(0)()
                    assert not work

        @block.scalar
        def _(act):
            def gates(c, j, s):
                z = pz[c][j // HALF][:, j % HALF, :, :].rearrange("p g b -> p (g b)")
                act.wait_ge(z_ready[c], s + 1)
                nc.scalar.activation(sg[c][:, :], z[:, 0:3 * NB], ACT.Sigmoid)
                nc.scalar.activation(gc[c][:, 0:NB], z[:, 3 * NB:4 * NB], ACT.Tanh).then_inc(gates_ready[c], 1)

            def tanh(c, s):
                act.wait_ge(cell_ready[c], s + 1)
                nc.scalar.activation(tc[c][:, :], gc[c][:, NB:2 * NB], ACT.Tanh).then_inc(tanh_ready[c], 1)

            with act.Fori(0, NBODY) as i:
                for j in range(BODY):
                    s = i * BODY + j
                    gates(X, j, s)
                    gates(Y, j, s)
                    tanh(X, s)
                    gates(Z, j, s)
                    tanh(Y, s)
                    tanh(Z, s)

        @block.vector
        def _(dve):
            for c in (X, Y, Z):
                nc.vector.memset(gc[c][:, NB:2 * NB], 0.0)
                nc.vector.memset(og[c][:, :], 0.0)
                nc.vector.memset(h[c][:, 1, 0, :], 0.0).then_inc(high_ready[c], 1)
                nc.vector.memset(h[c][:, 1, 1, :], 0.0).then_inc(low_ready[c], 1)
            nc.vector.memset(hist[:, :, :, :], 0.0).then_inc(state_zero, 1)
            dve.wait_ge(weights_in, 16 * 6)
            nc.vector.tensor_copy(u0[:, 0, :, :], u0f[:, :, :]).then_inc(split_done, 1)
            nc.vector.tensor_copy(u1[:, 0, :], u1f[:, :]).then_inc(split_done, 1)
            dve.wait_ge(split_done, 2)
            nc.vector.tensor_tensor(u0[:, 1, :, :], u0f[:, :, :], u0[:, 0, :, :], ALU.subtract).then_inc(split_done, 1)
            nc.vector.tensor_tensor(u1[:, 1, :], u1f[:, :], u1[:, 0, :], ALU.subtract).then_inc(split_done, 1)
            dve.wait_ge(state_zero, 1)

            def products(c, s):
                dve.wait_ge(gates_ready[c], s + 1)
                nc.vector.tensor_tensor(pr[c][:, :], sg[c][:, 0:2 * NB], gc[c][:, :], ALU.mult)\
                    .then_inc(products_ready[c], 1)

            def cell(c, s):
                dve.wait_ge(products_ready[c], s + 1)
                nc.vector.tensor_tensor(gc[c][:, NB:2 * NB], pr[c][:, 0:NB], pr[c][:, NB:2 * NB], ALU.add)\
                    .then_inc(cell_ready[c], 1)

            def keep_o(c, j):
                nc.vector.copy_predicated(og[c][:, :], mask[:, c // Z, j, :], sg[c][:, 2 * NB:3 * NB])

            def high(c, j, s):
                dve.wait_ge(tanh_ready[c], s + 1)
                nc.vector.tensor_tensor(h[c][:, j % 2, 0, :], og[c][:, :], tc[c][:, :], ALU.mult)\
                    .then_inc(high_ready[c], 1)

            def full(c, j):
                nc.vector.tensor_tensor(hist[:, c, (j - 1) % BODY, :], og[c][:, :], tc[c][:, :], ALU.mult)\
                    .then_inc(full_ready[c], 1)

            def low(c, j, s):
                dve.wait_ge(full_ready[c], s + 1)
                nc.vector.tensor_tensor(h[c][:, j % 2, 1, :], hist[:, c, (j - 1) % BODY, :], h[c][:, j % 2, 0, :],
                                        ALU.subtract).then_inc(low_ready[c], 1)

            with dve.Fori(0, NBODY) as i:
                for j in range(BODY):
                    s = i * BODY + j
                    if j % HALF == 0:
                        dve.wait_ge(mask_ready, i * 4 + 2 * (j // HALF) + 2)
                    if j % HALF == 1:
                        dve.wait_ge(lat_copied, i * 2 + j // HALF + 1)
                    products(X, s)
                    keep_o(X, j)
                    cell(X, s)
                    products(Y, s)
                    keep_o(Y, j)
                    high(X, j, s)
                    full(X, j)
                    cell(Y, s)
                    low(X, j, s)
                    products(Z, s)
                    keep_o(Z, j)
                    high(Y, j, s)
                    full(Y, j)
                    cell(Z, s)
                    low(Y, j, s)
                    high(Z, j, s)
                    full(Z, j)
                    low(Z, j, s)


def mixture(nc, tokens, ident, LAT, LAT0, ln_g, ln_b, wg_group, wg_inner, W1, b1, W2, b2, gln_g, gln_b, out, T, TP):
    G, E, _, FH = W1.shape
    HC = FH // P
    NTILE = TP // BODY
    NGATE = G + 1
    NLN = 2 + G
    with ExitStack() as ctx:
        def sb(name, shape, dt=F32):
            return ctx.enter_context(nc.sbuf_tensor(name, shape, dt))

        def psum(name):
            return ctx.enter_context(nc.psum_tensor(name, [P, 512], F32))

        def sem(name):
            return ctx.enter_context(nc.semaphore(name))

        w1 = sb("w1e", [P, G * E, FH])
        w2 = sb("w2e", [P, G * E, HC, P])
        b1r = sb("b1r", [G * E * HC, P])
        b1c = sb("b1c", [P, G * E, HC])
        b2s = sb("b2s", [E, G, P])
        wg = sb("wg", [P, G])
        wi = sb("wi", [P, G, E])
        vec = sb("vec", [P, 2 + 2 * G, P])
        iota = sb("iota", [P, NGATE, E])
        iotau = sb("iotau", [P, NGATE, E], U32)
        eps = sb("eps_e", [P, 1])
        ht = sb("ht", [P, P])
        latc = sb("latc", [P, P])
        h1 = sb("h1", [P, P])
        xf = sb("xf", [P, P])
        z = sb("z", [P, P])
        tmp = sb("tmp", [P, P])
        xfT = sb("xfT", [P, P])
        zT = sb("zT", [P, P])
        stats = sb("stats_e", [P, 6])
        mv = sb("mv_e", [P, 2])
        std = sb("std_e", [P, 1])
        rstd = sb("rstd_e", [P, 1])
        lg = sb("lg", [P, NGATE, E])
        top = sb("top", [P, NGATE, 8])
        ix = sb("ix", [P, NGATE, 8], U32)
        ixf = sb("ixf", [P, NGATE, 8])
        gap = sb("gap", [P, NGATE])
        p1 = sb("p1", [P, NGATE])
        p2 = sb("p2", [P, NGATE])
        m1 = sb("m1", [P, NGATE, E])
        m2 = sb("m2", [P, NGATE, E])
        wt = sb("wt", [P, NGATE, E])
        wtT = sb("wtT", [E, G, P])
        hid = [sb(f"hid{u}", [P, HC, P]) for u in range(2)]
        moe = sb("moe", [P, P])
        acc = sb("acc", [P, P])
        res = sb("res", [P, P])
        pH = [psum("pH0"), psum("pH1")]
        pO = [psum("pO0"), psum("pO1")]
        pA = psum("pA")
        pB = psum("pB")
        pL = psum("pL")
        pM = psum("pM")

        weights_in = sem("eweights_in")
        consts = sem("econsts")
        b1_turned = sem("b1_turned")
        b1_done = sem("b1_done")
        tile_in = sem("etile_in")
        lat_cut = sem("lat_cut")
        lat_turned = sem("lat_turned")
        h1_done = sem("h1_done")
        stats_done = sem("estats_done")
        mv_done = sem("emv_done")
        std_done = sem("estd_done")
        rstd_done = sem("erstd_done")
        norm_done = sem("norm_done")
        scaled = sem("scaled")
        z_done = sem("z_done")
        x_turned = sem("x_turned")
        xT_done = sem("xT_done")
        logits = sem("logits")
        lg_done = sem("lg_done")
        top_done = sem("top_done")
        gap_done = sem("gap_done")
        p_done = sem("p_done")
        eq_done = sem("eq_done")
        wt_done = sem("wt_done")
        wt_turned = sem("wt_turned")
        wtT_done = sem("wtT_done")
        bias_ready = sem("bias_ready")
        moe_done = sem("moe_done")
        up_ready = sem("up_ready")
        hid_done = [sem("hid_done_a"), sem("hid_done_v")]
        down_ready = sem("down_ready")
        mixed = sem("mixed")
        acc_done = sem("acc_done")
        acc_sum = sem("acc_sum")
        res_done = sem("res_done")
        res_out = sem("res_out")
        block = ctx.enter_context(nc.Block())
        NEXP = G * E

        def bc(v):
            return v.rearrange("(a d) -> a d", a=1).to_broadcast([P, P])

        @block.sync
        def _(sp):
            sp.dma_start(b1r[:, :], b1.rearrange("g e (c p) -> (g e c) p", p=P)).then_inc(weights_in, 16)
            sp.dma_start(b2s[:, :, :], b2.rearrange("g e d -> e g d")).then_inc(weights_in, 16)
            sp.dma_start(wg[:, :], wg_group).then_inc(weights_in, 16)
            sp.dma_start(wi[:, :, :], wg_inner.rearrange("g d e -> d g e")).then_inc(weights_in, 16)
            sp.dma_start(vec[:, 0, :], bc(ln_g)).then_inc(weights_in, 16)
            sp.dma_start(vec[:, 1, :], bc(ln_b)).then_inc(weights_in, 16)
            for g in range(G):
                sp.dma_start(vec[:, 2 + 2 * g, :], bc(gln_g[g])).then_inc(weights_in, 16)
                sp.dma_start(vec[:, 3 + 2 * g, :], bc(gln_b[g])).then_inc(weights_in, 16)
            sp.dma_start(w1[:, :, :], W1.rearrange("g e d h -> d (g e) h")).then_inc(weights_in, 16)
            sp.dma_start(w2[:, :, :, :].rearrange("p n c d -> p (n c) d"),
                         W2.rearrange("g e (c p) d -> p (g e c) d", p=P)).then_inc(weights_in, 16)
            tiles = tokens.rearrange("(n t) b d -> n (t b) d", t=BODY)

            def load(i):
                sp.wait_ge(h1_done, i + 1)
                sp.dma_start(ht[:, :], tiles[bass.ds(i, 1)].rearrange("n p d -> (n p) d")).then_inc(tile_in, 16)

            def store(i, n):
                sp.wait_ge(res_done, i + 1)
                for b in range(NB):
                    sp.dma_start(out[b, bass.ds(i * BODY, n), :], res[b:n * NB:NB, :]).then_inc(res_out, 16)

            with sp.Fori(0, NTILE - 1) as i:
                load(i)
                store(i, BODY)
            load(NTILE - 1)
            store(NTILE - 1, T - (NTILE - 1) * BODY)
            sp.wait_ge(res_out, 16 * NB * (NTILE + 1))

        @block.gpsimd
        def _(pool):
            pool.iota(iotau[:, :, :], pattern=[[0, NGATE], [1, E]], base=0, channel_multiplier=0).then_inc(consts, 1)
            pool.memset(eps[:, :], EPS).then_inc(consts, 1)
            pool.memset(lg[:, 0, :], -3e38).then_inc(consts, 1)

        @block.tensor
        def _(pe):
            pe.wait_ge(weights_in, 16 * (8 + 2 * G))
            pe.matmul(pA[:, 0:P], b1r[:, :], ident[:, :], start=True, stop=True).then_inc(b1_turned, 1)
            pe.wait_ge(b1_done, 1)
            with pe.Fori(0, NTILE) as i:
                pe.wait_ge(lat_cut, i + 1)
                pe.transpose(pA[:, 0:P], latc[:, :], ident[:, :]).then_inc(lat_turned, 1)
                pe.wait_ge(z_done, i + 1)
                pe.transpose(pA[:, 0:P], xf[:, :], ident[:, :])
                pe.transpose(pB[:, 0:P], z[:, :], ident[:, :]).then_inc(x_turned, 1)
                pe.wait_ge(xT_done, i + 1)
                pe.matmul(pL[:, 0:G], xfT[:, :], wg[:, :], start=True, stop=True)
                pe.matmul(pL[:, E:E + G * E], zT[:, :], wi[:, :, :].rearrange("p g e -> p (g e)"), start=True, stop=True)\
                    .then_inc(logits, 1)
                pe.wait_ge(wt_done, i + 1)
                for g in range(G):
                    mm = pe.matmul(pB[0:E, g * P:(g + 1) * P], wt[:, 1 + g, :], ident[:, :], start=True, stop=True)
                mm.then_inc(wt_turned, 1)
                pe.wait_ge(wtT_done, i + 1)

                def up(n):
                    for c in range(HC):
                        mm = pe.matmul(pH[n % 2][:, c * P:(c + 1) * P], w1[:, n, c * P:(c + 1) * P], zT[:, :],
                                       start=True, stop=True)
                    mm.then_inc(up_ready, 1)

                def down(n):
                    pe.wait_ge(hid_done[n % 2], i * (NEXP // 2) + n // 2 + 1)
                    pe.wait_ge(mixed, i * NEXP + n + 1)
                    for c in range(HC):
                        mm = pe.matmul(pO[n % 2][:, 0:P], hid[n % 2][:, c, :], w2[:, n, c, :],
                                       start=(c == 0), stop=(c == HC - 1))
                    mm.then_inc(down_ready, 1)

                for n in range(NEXP + 1):
                    if n < NEXP:
                        if n % E == 0:
                            g = n // E
                            pe.wait_ge(moe_done, i * G + g + 1)
                            pe.matmul(pM[:, 0:P], wtT[:, g, :], b2s[:, g, :], start=True, stop=True)\
                                .then_inc(bias_ready, 1)
                        up(n)
                    if n:
                        down(n - 1)

        @block.scalar
        def _(act):
            act.wait_ge(b1_turned, 1)
            nc.scalar.copy(b1c[:, :, :].rearrange("p n c -> p (n c)"), pA[:, 0:P]).then_inc(b1_done, 1)
            act.wait_ge(consts, 3)

            def root(n):
                act.wait_ge(mv_done, n + 1)
                nc.scalar.activation(std[:, :], mv[:, 1:2], ACT.Sqrt, bias=eps[:, :]).then_inc(std_done, 1)

            with act.Fori(0, NTILE) as i:
                nc.scalar.copy(latc[:, :], LAT[:, bass.ds((i * BODY + LAT0) * NB, NT)]).then_inc(lat_cut, 1)
                root(i * NLN)
                root(i * NLN + 1)
                act.wait_ge(x_turned, i + 1)
                nc.scalar.copy(xfT[:, :], pA[:, 0:P])
                nc.scalar.copy(zT[:, :], pB[:, 0:P]).then_inc(xT_done, 1)
                act.wait_ge(gap_done, i + 1)
                nc.scalar.activation(p1[:, :], gap[:, :], ACT.Sigmoid)
                nc.scalar.activation(p2[:, :], gap[:, :], ACT.Sigmoid, scale=-1.0).then_inc(p_done, 1)
                act.wait_ge(wt_turned, i + 1)
                nc.scalar.copy(wtT[:, :, :].rearrange("p g n -> p (g n)"), pB[0:E, 0:G * P]).then_inc(wtT_done, 1)
                for n in range(NEXP):
                    if n % 2 == 0:
                        act.wait_ge(up_ready, i * NEXP + n + 1)
                        for c in range(HC):
                            ins = nc.scalar.activation(hid[0][:, c, :], pH[0][:, c * P:(c + 1) * P], ACT.Relu,
                                                       bias=b1c[:, n, c:c + 1])
                        ins.then_inc(hid_done[0], 1)
                    if n % E == E - 1:
                        root(i * NLN + 2 + n // E)

        @block.vector
        def _(dve):
            dve.sem_inc(h1_done, 1)
            dve.sem_inc(mixed, TOKENS - 1)
            dve.sem_inc(moe_done, 1)
            dve.sem_inc(acc_done, 1)
            dve.sem_inc(res_out, 16 * NB)
            dve.wait_ge(consts, 3)
            nc.vector.tensor_copy(iota[:, :, :], iotau[:, :, :])
            dve.wait_ge(b1_done, 1)
            dve.wait_ge(weights_in, 16 * (8 + 2 * G))

            def norm(n, to, src):
                nc.vector.bn_stats(stats[:, :], src).then_inc(stats_done, 1)
                dve.wait_ge(stats_done, n + 1)
                nc.vector.memset(rstd[:, :], 0.0)
                nc.vector.bn_aggr(mv[:, :], stats[:, :]).then_inc(mv_done, 1)
                dve.wait_ge(std_done, n + 1)
                nc.vector.reciprocal(rstd[:, :], std[:, :]).then_inc(rstd_done, 1)
                dve.wait_ge(rstd_done, n + 1)
                nc.vector.tensor_scalar(to, src, mv[:, 0:1], rstd[:, :], ALU.subtract, ALU.mult).then_inc(norm_done, 1)
                dve.wait_ge(norm_done, n + 1)

            def affine(n, to, src, v):
                nc.vector.tensor_tensor(tmp[:, :], src, vec[:, v, :], ALU.mult).then_inc(scaled, 1)
                dve.wait_ge(scaled, n + 1)
                return nc.vector.tensor_tensor(to, tmp[:, :], vec[:, v + 1, :], ALU.add)

            def wide(a):
                return a.rearrange("p (g a) -> p g a", a=1).to_broadcast([P, NGATE, E])

            with dve.Fori(0, NTILE) as i:
                dve.wait_ge(tile_in, 16 * i + 16)
                dve.wait_ge(lat_turned, i + 1)
                nc.vector.tensor_tensor(h1[:, :], ht[:, :], pA[:, 0:P], ALU.add).then_inc(h1_done, 1)
                dve.wait_ge(h1_done, i + 2)
                norm(i * NLN, xf[:, :], h1[:, :])
                norm(i * NLN + 1, z[:, :], xf[:, :])
                affine(i * (1 + G), z[:, :], z[:, :], 0).then_inc(z_done, 1)
                dve.wait_ge(logits, i + 1)
                nc.vector.tensor_copy(lg[:, 0, 0:G], pL[:, 0:G])
                nc.vector.tensor_copy(lg[:, 1:, :].rearrange("p g e -> p (g e)"), pL[:, E:E + G * E])\
                    .then_inc(lg_done, 1)
                dve.wait_ge(lg_done, i + 1)
                nc.vector.memset(gap[:, :], 0.0)
                for g in range(NGATE):
                    ins = nc.vector.max(top[:, g, :], lg[:, g, :])
                ins.then_inc(top_done, 1)
                dve.wait_ge(top_done, 3 * i + 1)
                nc.vector.tensor_tensor(gap[:, :], top[:, :, 0], top[:, :, 1], ALU.subtract).then_inc(gap_done, 1)
                for g in range(NGATE):
                    ins = nc.vector.max_index(ix[:, g, :], top[:, g, :], lg[:, g, :])
                ins.then_inc(top_done, 1)
                dve.wait_ge(top_done, 3 * i + 2)
                nc.vector.tensor_copy(ixf[:, :, :], ix[:, :, :]).then_inc(top_done, 1)
                dve.wait_ge(top_done, 3 * i + 3)
                dve.wait_ge(p_done, i + 1)
                nc.vector.tensor_tensor(m1[:, :, :], iota[:, :, :], wide(ixf[:, :, 0]), ALU.is_equal)
                nc.vector.tensor_tensor(m2[:, :, :], iota[:, :, :], wide(ixf[:, :, 1]), ALU.is_equal).then_inc(eq_done, 1)
                dve.wait_ge(eq_done, 2 * i + 1)
                nc.vector.tensor_tensor(m1[:, :, :], m1[:, :, :], wide(p1[:, :]), ALU.mult)
                nc.vector.tensor_tensor(m2[:, :, :], m2[:, :, :], wide(p2[:, :]), ALU.mult).then_inc(eq_done, 1)
                dve.wait_ge(eq_done, 2 * i + 2)
                nc.vector.tensor_tensor(wt[:, :, :], m1[:, :, :], m2[:, :, :], ALU.add).then_inc(wt_done, 1)
                dve.wait_ge(wt_done, i + 1)

                def mix(n):
                    dve.wait_ge(down_ready, i * NEXP + n + 1)
                    dve.wait_ge(mixed, i * NEXP + n + 1)
                    nc.vector.scalar_tensor_tensor(out=moe[:, :], in0=pO[n % 2][:, 0:P],
                                                   scalar=wt[:, 1 + n // E, n % E:n % E + 1],
                                                   in1=moe[:, :], op0=ALU.mult, op1=ALU.add).then_inc(mixed, 1)

                for n in range(NEXP):
                    g = n // E
                    if n % E == 0:
                        dve.wait_ge(bias_ready, i * G + g + 1)
                        dve.wait_ge(acc_done, i * 2 * G + 2 * g + 1)
                        nc.vector.tensor_tensor(moe[:, :], z[:, :], pM[:, 0:P], ALU.add).then_inc(moe_done, 1)
                        dve.wait_ge(moe_done, i * G + g + 2)
                    if n % 2 == 1:
                        dve.wait_ge(up_ready, i * NEXP + n + 1)
                        for c in range(HC):
                            ins = nc.vector.tensor_scalar(hid[1][:, c, :], pH[1][:, c * P:(c + 1) * P],
                                                          b1c[:, n, c:c + 1], 0.0, ALU.add, ALU.max)
                        ins.then_inc(hid_done[1], 1)
                        mix(n - 1)
                        mix(n)
                        if n % E == E - 1:
                            dve.wait_ge(mixed, i * NEXP + n + 2)
                            norm(i * NLN + 2 + g, moe[:, :], moe[:, :])
                            affine(i * (1 + G) + 1 + g, moe[:, :], moe[:, :], 2 + 2 * g).then_inc(acc_done, 1)
                            dve.wait_ge(acc_done, i * 2 * G + 2 * g + 2)
                            if g == 0:
                                nc.vector.tensor_scalar(acc[:, :], moe[:, :], wt[:, 0, g:g + 1], None, ALU.mult)\
                                    .then_inc(acc_done, 1)
                            else:
                                nc.vector.scalar_tensor_tensor(out=acc[:, :], in0=moe[:, :], scalar=wt[:, 0, g:g + 1],
                                                               in1=acc[:, :], op0=ALU.mult, op1=ALU.add)\
                                    .then_inc(acc_done, 1)
                dve.wait_ge(acc_done, i * 2 * G + 2 * G + 1)
                nc.vector.tensor_tensor(tmp[:, :], acc[:, :], xf[:, :], ALU.add).then_inc(acc_sum, 1)
                dve.wait_ge(acc_sum, i + 1)
                dve.wait_ge(res_out, 16 * NB * (i + 1))
                nc.vector.tensor_tensor(res[:, :], tmp[:, :], h1[:, :], ALU.add).then_inc(res_done, 1)


def fusion_kernel(nc, x, txt, tok_W, tok_b, tok_cls, W0, U0, b0, W1, U1, b1, ln_g, ln_b, wg_group, wg_inner,
                  fW1, fb1, fW2, fb2, gln_g, gln_b, out):
    T = 1 + (x.shape[2] // 4) * (x.shape[3] // 4) + txt.shape[1]
    assert x.shape[0] == NB and txt.shape[2] == P and (T + LAG) % BODY == 0
    NBODY = (T + LAG) // BODY
    TP = NBODY * BODY
    TX = TP + HALF
    LAT0 = LAG - 1 + HALF
    tokens = nc.dram_tensor("tokens", [TP, NB, P], F32, kind="Internal").ap()
    with ExitStack() as ctx:
        def sb(name, shape, dt=F32):
            return ctx.enter_context(nc.sbuf_tensor(name, shape, dt))

        ident = sb("ident", [P, P])
        LAT = sb("LAT", [P, (TP + LAT0) * NB])
        with ExitStack() as inner:
            XNT = inner.enter_context(nc.sbuf_tensor("XNT", [P, TX * NB], F32))
            CNT = inner.enter_context(nc.sbuf_tensor("CNT", [P, (LAG + TX) * NB], U16))
            RHS = inner.enter_context(nc.sbuf_tensor("RHS", [2, (LAG + TX) * NB], F32))
            make_tokens(nc, tokens, ident, XNT, CNT, RHS, x, txt, tok_W, tok_b, tok_cls, T, TP)
            recur(nc, XNT, CNT, RHS, LAT, W0, U0, b0, W1, U1, b1, NBODY)
        mixture(nc, tokens, ident, LAT, LAT0, ln_g, ln_b, wg_group, wg_inner, fW1, fb1, fW2, fb2, gln_g, gln_b,
                out, T, TP)


_INS = ['x', 'txt', 'L0_tok_W', 'L0_tok_b', 'L0_tok_cls', 'L0_attn_W0', 'L0_attn_U0', 'L0_attn_b0', 'L0_attn_W1',
        'L0_attn_U1', 'L0_attn_b1', 'L0_ffn_ln_g', 'L0_ffn_ln_b', 'L0_ffn_wg_group', 'L0_ffn_wg_inner', 'L0_ffn_W1',
        'L0_ffn_b1', 'L0_ffn_W2', 'L0_ffn_b2', 'L0_ffn_gln_g', 'L0_ffn_gln_b']


def kernel(**inputs):
    import numpy as _np
    import concourse.bacc as _bacc
    from concourse import mybir as _mybir
    from concourse.bass_utils import run_bass_kernel_spmd as _run

    nc = _bacc.Bacc("TRN2", target_bir_lowering=False, num_devices=1)
    arrays, args = {}, []
    for name in _INS:
        a = _np.ascontiguousarray(inputs[name])
        arrays[f"in_{name}_dram"] = a
        args.append(nc.dram_tensor(f"in_{name}_dram", a.shape, _mybir.dt.from_np(a.dtype), kind="ExternalInput").ap())
    x, txt = inputs['x'], inputs['txt']
    shape = (x.shape[0], 1 + (x.shape[2] // 4) * (x.shape[3] // 4) + txt.shape[1], txt.shape[2])
    out = nc.dram_tensor("out_0_dram", shape, _mybir.dt.float32, kind="ExternalOutput").ap()
    fusion_kernel(nc, *args, out)
    r = _run(nc, [arrays], core_ids=[0])
    return r.results[0]["out_0_dram"]
```

```python
from contextlib import ExitStack

import concourse.bass as bass
from concourse import mybir

ALU = mybir.AluOpType
ACT = mybir.ActivationFunctionType
F32 = mybir.dt.float32
F16 = mybir.dt.float16
BF16 = mybir.dt.bfloat16
U16 = mybir.dt.uint16
U32 = mybir.dt.uint32

P = 128
NB = 2
EPS = 1e-5
SAT = 32768.0
WSCALE = 64.0
FSCALE = 16.0
BODY = 64
HALF = BODY // 2
LAG = BODY - 1
NT = NB * BODY
GATES = (1, 0, 3, 2)
X, Y, Z = range(3)


TOKENS = 2


def done(n):
    return n + 1 + TOKENS


def freed(n):
    return n + 1


def make_tokens(nc, tokens, ident, XN, CNT, RHS, x, txt, tok_W, tok_b, tok_cls, T, TP):
    C, IH, IW = x.shape[1:]
    PS = 4
    GI, GJ = IH // PS, IW // PS
    KP = C * PS * PS
    NR = NB * GI
    NTILE = TP // BODY
    assert GJ % 2 == 0 and NTILE % 2 == 0
    with ExitStack() as ctx:
        def sb(name, shape, dt=F32):
            return ctx.enter_context(nc.sbuf_tensor(name, shape, dt))

        def psum(name):
            return ctx.enter_context(nc.psum_tensor(name, [P, 512], F32))

        def sem(name):
            return ctx.enter_context(nc.semaphore(name))

        img = sb("img", [NR, C * PS, IW])
        wtok = sb("wtok", [P, KP])
        wtokT = sb("wtokT", [KP, P])
        btok = sb("btok", [NR, P])
        patch = sb("patch", [NR, 2, KP])
        patchT = sb("patchT", [KP, 2, NR])
        emb = sb("emb", [NR, 2, P])
        zrow = sb("zrow", [NT, P])
        tile = sb("tile", [P, 2, P])
        xn = sb("xn", [P, 2, P])
        stats = sb("stats", [P, 2, 6])
        mv = sb("mv", [P, 2, 2])
        std = sb("std", [P, 2])
        rstd = sb("rstd", [P, 2])
        eps = sb("eps", [P, 1])
        ones = sb("ones", [P, P], BF16)
        live = sb("live", [P, 2, P], BF16)
        dead = sb("dead", [1, RHS.shape[1]], F16)
        pT = [psum("pT0"), psum("pT1")]
        pE = [psum("pE0"), psum("pE1")]
        pX = [psum("pX0"), psum("pX1")]
        pC = [psum("pC0"), psum("pC1")]

        inputs_in = sem("inputs_in")
        consts_done = sem("consts_done")
        ident_done = sem("ident_done")
        pads_done = sem("pads_done")
        rest_out = sem("rest_out")
        patch_cut = sem("patch_cut")
        patch_turned = sem("patch_turned")
        patchT_done = sem("patchT_done")
        emb_made = sem("emb_made")
        emb_done = sem("emb_done")
        emb_out = [sem("emb_out0"), sem("emb_out1")]
        wtok_turned = sem("wtok_turned")
        wtokT_done = sem("wtokT_done")
        tile_in = [sem("tile_in0"), sem("tile_in1")]
        stats_done = sem("stats_done")
        mv_done = sem("mv_done")
        std_done = sem("std_done")
        rstd_done = sem("rstd_done")
        xn_done = sem("xn_done")
        xn_turned = sem("xn_turned")
        xnt_done = sem("xnt_done")
        low_done = sem("low_done")
        counted = sem("counted")
        dead_done = sem("dead_done")
        dead_out = sem("dead_out")
        block = ctx.enter_context(nc.Block())

        emb_rows = tokens[1:1 + GI * GJ, :, :].rearrange("(i j) b d -> b i j d", j=GJ)
        tiles = tokens.rearrange("(n t) b d -> n (t b) d", t=BODY)

        @block.sync
        def _(sp):
            for b in range(NB):
                for c in range(C):
                    sp.dma_start(img[b * GI:(b + 1) * GI, c * PS:(c + 1) * PS, :],
                                 x[b, c].rearrange("(i p) w -> i p w", p=PS)).then_inc(inputs_in, 16)
            sp.dma_start(wtok[:, :], tok_W).then_inc(inputs_in, 16)
            sp.dma_start(btok[:, :], tok_b.rearrange("(a d) -> a d", a=1).to_broadcast([NR, P]))\
                .then_inc(inputs_in, 16)
            for b in range(NB):
                sp.dma_start(tokens[1 + GI * GJ:T, b, :], txt[b]).then_inc(rest_out, 16)
                sp.dma_start(tokens[0:1, b, :], tok_cls[0]).then_inc(rest_out, 16)
            sp.wait_ge(consts_done, 3)
            sp.dma_start(tokens[T:TP].rearrange("t b d -> (t b) d"), zrow[0:(TP - T) * NB, :]).then_inc(rest_out, 16)
            sp.dma_start(tokens[TP:TP + BODY].rearrange("t b d -> (t b) d"), zrow[:, :]).then_inc(rest_out, 16)
            with sp.Fori(0, GJ // 2) as pair:
                j = 2 * pair
                for u in range(2):
                    sp.wait_ge(emb_done, done(j + u))
                    for b in range(NB):
                        sp.dma_start(emb_rows[b, :, bass.ds(j + u, 1), :].rearrange("i a d -> i (a d)"),
                                     emb[b * GI:(b + 1) * GI, u, :]).then_inc(emb_out[u], 16)
            sp.wait_ge(rest_out, 16 * (2 * NB + 2))
            for u in range(2):
                sp.wait_ge(emb_out[u], 16 * NB * (GJ // 2 + 1))
            with sp.Fori(0, NTILE // 2) as pair:
                i = 2 * pair
                for u in range(2):
                    sp.wait_ge(xn_done, freed(i + u))
                    sp.dma_start(tile[:, u, :], tiles[bass.ds(i + u, 1)].rearrange("n p d -> (n p) d"))\
                        .then_inc(tile_in[u], 16)
            sp.wait_ge(dead_done, NTILE + TOKENS)
            sp.wait_ge(pads_done, 6)
            sp.dma_start(RHS[2:3, :], dead[:, :]).then_inc(dead_out, 16)
            sp.wait_ge(dead_out, 16)

        @block.gpsimd
        def _(pool):
            pool.memset(zrow[:, :], 0.0).then_inc(consts_done, 1)
            pool.memset(eps[:, :], EPS).then_inc(consts_done, 1)
            pool.memset(ones[:, :], 1.0).then_inc(consts_done, 1)
            pool.memset(ident[:, :], 0.0).then_inc(ident_done, 1)
            pool.wait_ge(ident_done, 1)
            pool.affine_select(out=ident[:, :], in_=ident[:, :], compare_op=ALU.not_equal, fill=1.0, base=0,
                               pattern=[[-1, P]], channel_multiplier=1).then_inc(ident_done, 1)
            pool.memset(CNT[:, 0:LAG * NB], 0.0).then_inc(pads_done, 1)
            pool.memset(CNT[:, (LAG + TP) * NB:], 0.0).then_inc(pads_done, 1)
            pool.memset(dead[:, 0:LAG * NB], WSCALE).then_inc(pads_done, 1)
            pool.memset(dead[:, (LAG + TP) * NB:], WSCALE).then_inc(pads_done, 1)
            pool.memset(XN[:, :, TP * NB:], 0.0).then_inc(pads_done, 1)
            pool.memset(RHS[0:2, :], 1.0).then_inc(pads_done, 1)

        @block.tensor
        def _(pe):
            pe.sem_inc(patch_turned, TOKENS)
            pe.sem_inc(emb_made, TOKENS)
            pe.sem_inc(xn_turned, TOKENS)
            pe.sem_inc(counted, TOKENS)
            pe.wait_ge(ident_done, 2)
            pe.wait_ge(inputs_in, 16 * (NB * C + 2))
            pe.transpose(pE[0][0:KP, 0:P], wtok[:, :], ident[:, :]).then_inc(wtok_turned, 1)
            pe.wait_ge(wtokT_done, 1)
            with pe.Fori(0, GJ // 2) as pair:
                j = 2 * pair
                for u in range(2):
                    pe.wait_ge(patch_cut, j + u + 1)
                    pe.wait_ge(patchT_done, freed(j + u))
                    pe.matmul(pT[u][0:KP, 0:NR], patch[:, u, :], ident[0:NR, 0:NR], start=True, stop=True)\
                        .then_inc(patch_turned, 1)
                for u in range(2):
                    pe.wait_ge(patchT_done, done(j + u))
                    pe.wait_ge(emb_done, freed(j + u))
                    pe.matmul(pE[u][0:NR, 0:P], patchT[:, u, :], wtokT[:, :], start=True, stop=True)\
                        .then_inc(emb_made, 1)
            with pe.Fori(0, NTILE // 2) as pair:
                i = 2 * pair
                for u in range(2):
                    pe.wait_ge(xn_done, done(i + u))
                    pe.wait_ge(low_done, freed(i + u))
                    pe.transpose(pX[u][:, 0:P], xn[:, u, :], ident[:, :]).then_inc(xn_turned, 1)
                for u in range(2):
                    pe.wait_ge(low_done, done(i + u))
                    pe.wait_ge(dead_done, freed(i + u))
                    pe.matmul(pC[u][:, 0:P], ones[:, :], live[:, u, :], start=True, stop=True).then_inc(counted, 1)

        @block.scalar
        def _(act):
            act.sem_inc(patchT_done, TOKENS)
            act.sem_inc(xnt_done, TOKENS)
            act.wait_ge(wtok_turned, 1)
            nc.scalar.copy(wtokT[:, :], pE[0][0:KP, 0:P]).then_inc(wtokT_done, 1)
            with act.Fori(0, GJ // 2) as pair:
                j = 2 * pair
                for u in range(2):
                    act.wait_ge(patch_turned, done(j + u))
                    act.wait_ge(emb_made, freed(j + u))
                    nc.scalar.copy(patchT[:, u, :], pT[u][0:KP, 0:NR]).then_inc(patchT_done, 1)
            act.wait_ge(consts_done, 3)
            with act.Fori(0, NTILE // 2) as pair:
                i = 2 * pair
                for u in range(2):
                    act.wait_ge(mv_done, i + u + 1)
                    nc.scalar.activation(std[:, u:u + 1], mv[:, u, 1:2], ACT.Sqrt, bias=eps[:, :])\
                        .then_inc(std_done, 1)
                for u in range(2):
                    act.wait_ge(xn_turned, done(i + u))
                    nc.scalar.copy(XN[:, 0, bass.ds((i + u) * NT, NT)], pX[u][:, 0:P]).then_inc(xnt_done, 1)

        @block.vector
        def _(dve):
            dve.sem_inc(emb_done, TOKENS)
            dve.sem_inc(xn_done, TOKENS)
            dve.sem_inc(dead_done, TOKENS)
            dve.sem_inc(low_done, TOKENS)
            for u in range(2):
                dve.sem_inc(emb_out[u], NB * 16)
            dve.wait_ge(inputs_in, 16 * (NB * C + 2))
            with dve.Fori(0, GJ // 2) as pair:
                j = 2 * pair
                for u in range(2):
                    dve.wait_ge(patch_turned, freed(j + u))
                    nc.vector.tensor_copy(patch[:, u, :].rearrange("p (r w) -> p r w", w=PS),
                                          img[:, :, bass.ds((j + u) * PS, PS)]).then_inc(patch_cut, 1)
                for u in range(2):
                    dve.wait_ge(emb_made, done(j + u))
                    dve.wait_ge(emb_out[u], NB * 16 * (pair + 1))
                    nc.vector.tensor_tensor(emb[:, u, :], pE[u][0:NR, 0:P], btok[:, :], ALU.add)\
                        .then_inc(emb_done, 1)
            dve.wait_ge(consts_done, 3)
            with dve.Fori(0, NTILE // 2) as pair:
                i = 2 * pair
                for u in range(2):
                    dve.wait_ge(tile_in[u], 8 * i + 16)
                    nc.vector.bn_stats(stats[:, u, :], tile[:, u, :]).then_inc(stats_done, 1)
                for u in range(2):
                    dve.wait_ge(stats_done, i + u + 1)
                    nc.vector.memset(rstd[:, u:u + 1], 0.0)
                    nc.vector.bn_aggr(mv[:, u, :], stats[:, u, :]).then_inc(mv_done, 1)
                for u in range(2):
                    dve.wait_ge(std_done, i + u + 1)
                    nc.vector.reciprocal(rstd[:, u:u + 1], std[:, u:u + 1]).then_inc(rstd_done, 1)
                for u in range(2):
                    dve.wait_ge(rstd_done, i + u + 1)
                    dve.wait_ge(xn_turned, freed(i + u))
                    nc.vector.tensor_scalar(xn[:, u, :], tile[:, u, :], mv[:, u, 0:1], rstd[:, u:u + 1],
                                            ALU.subtract, ALU.mult).then_inc(xn_done, 1)
                for u in range(2):
                    dve.wait_ge(xnt_done, done(i + u))
                    dve.wait_ge(counted, freed(i + u))
                    nc.vector.tensor_scalar(live[:, u, :], pX[u][:, 0:P], 0.0, None, ALU.not_equal)
                    nc.vector.tensor_tensor(XN[:, 1, bass.ds((i + u) * NT, NT)], pX[u][:, 0:P],
                                            XN[:, 0, bass.ds((i + u) * NT, NT)], ALU.subtract).then_inc(low_done, 1)
                for u in range(2):
                    dve.wait_ge(counted, done(i + u))
                    nc.vector.tensor_copy(CNT[:, bass.ds((i + u) * NT + LAG * NB, NT)], pC[u][:, 0:P])
                    nc.vector.tensor_scalar(dead[:, bass.ds((i + u) * NT + LAG * NB, NT)], pC[u][0:1, 0:P], 0.0, WSCALE,
                                            ALU.is_equal, ALU.mult).then_inc(dead_done, 1)


def recur(nc, XN, CNT, RHS, LAT, W0, U0, b0, W1, U1, b1, NBODY):
    H0, H1 = U0.shape[0], U1.shape[0]
    NCOL = 4 * (H0 + H1)
    assert H0 == 2 * P and H1 == P
    CHAINS = (X, Y, Z)
    with ExitStack() as ctx:
        def sb(name, shape, dt=F32):
            return ctx.enter_context(nc.sbuf_tensor(name, shape, dt))

        def sem(name):
            return ctx.enter_context(nc.semaphore(name))

        def each(make, name):
            return [make(f"{name}{c}") for c in "XYZ"]

        full = [sb("w0f", [P, 1, 4 * H0]), sb("u0f", [P, 2, 4 * H0]), sb("w1f", [P, 2, 4 * H1]),
                sb("u1f", [P, 1, 4 * H1])]
        w0, u0, w1, u1 = [sb(n, [P, 2, *f.shape[1:]], F16) for n, f in zip(("w0", "u0", "w1", "u1"), full)]
        bw = sb("bw", [3, NCOL], F16)
        biasf = sb("biasf", [1, NCOL])
        blow = sb("blow", [1, NCOL], F16)
        satrow = sb("satrow", [1, NCOL], F16)
        hist = sb("hist", [P, 3, 2, BODY, NB], F16)
        states = sb("states", [P, BODY, NB])
        tg = each(lambda n: sb(n, [P, NB]), "tg")
        fio = each(lambda n: sb(n, [P, 3, NB, 2]), "fio")
        cig = each(lambda n: sb(n, [P, 2, 1 + 2 * NB]), "cig")
        og = each(lambda n: sb(n, [P, NB]), "og")
        tc = each(lambda n: sb(n, [P, NB]), "tc")
        new = each(lambda n: sb(n, [P, NB]), "new")
        mask = sb("mask", [P, 2, BODY, NB], U16)
        pz = [[ctx.enter_context(nc.psum_tensor(f"z{c}{p}", [P, HALF, 4, NB], F32)) for p in range(2)] for c in "XYZ"]

        weights_in = sem("weights_in")
        sat_done = sem("sat_done")
        high_split = sem("high_split")
        low_split = sem("low_split")
        rows_in = sem("rows_in")
        state_zero = sem("state_zero")
        input_ready = each(sem, "input_ready")
        gates_ready = each(sem, "gates_ready")
        product_ready = each(sem, "product_ready")
        cell_ready = each(sem, "cell_ready")
        tanh_ready = each(sem, "tanh_ready")
        high_ready = each(sem, "high_ready")
        full_ready = each(sem, "full_ready")
        low_ready = each(sem, "low_ready")
        mask_ready = sem("mask_ready")
        lat_copied = sem("lat_copied")
        block = ctx.enter_context(nc.Block())

        @block.sync
        def _(sp):
            for t, w in zip(full, (W0, U0, W1, U1)):
                sp.dma_start(t[:, :, :], w.rearrange("(k p) n -> p k n", p=P)).then_inc(weights_in, 16)
            sp.dma_start(biasf[0:1, 0:4 * H0], b0.rearrange("(a n) -> a n", a=1)).then_inc(weights_in, 16)
            sp.dma_start(biasf[0:1, 4 * H0:], b1.rearrange("(a n) -> a n", a=1)).then_inc(weights_in, 16)
            sp.wait_ge(sat_done, 5)
            sp.dma_start(bw[2:3, :], satrow[:, :]).then_inc(rows_in, 16)
            sp.wait_ge(low_split, 5)
            sp.dma_start(bw[1:2, :], blow[:, :]).then_inc(rows_in, 16)

        @block.gpsimd
        def _(pool):
            pool.memset(satrow[:, :], 0.0).then_inc(sat_done, 1)
            pool.wait_ge(sat_done, 1)
            for base, n in ((0, H0), (4 * H0, H1)):
                pool.memset(satrow[:, base:base + n], -SAT).then_inc(sat_done, 1)
                pool.memset(satrow[:, base + n:base + 2 * n], SAT).then_inc(sat_done, 1)

            def copy_masks(half, t0):
                nc.gpsimd.tensor_copy(mask[:, 0, half * HALF:(half + 1) * HALF, :].rearrange("p t b -> p (t b)"),
                                      CNT[:, bass.ds((t0 + LAG) * NB, HALF * NB)]).then_inc(mask_ready, 1)
                nc.gpsimd.tensor_copy(mask[:, 1, half * HALF:(half + 1) * HALF, :].rearrange("p t b -> p (t b)"),
                                      CNT[:, bass.ds(t0 * NB, HALF * NB)]).then_inc(mask_ready, 1)

            def copy_out(half, at):
                nc.gpsimd.tensor_copy(LAT[:, bass.ds(at * NB, HALF * NB)],
                                      states[:, half * HALF:(half + 1) * HALF, :].rearrange("p t b -> p (t b)"))\
                    .then_inc(lat_copied, 1)

            pool.sem_inc(lat_copied, 1)
            pool.memset(LAT[:, (NBODY * BODY + HALF) * NB:], 0.0)
            copy_masks(0, 0)
            with pool.Fori(0, NBODY) as i:
                s0 = i * BODY
                pool.wait_ge(low_ready[Z], s0 + 1)
                copy_masks(1, s0 + HALF)
                pool.wait_ge(low_ready[Z], s0 + 2)
                copy_out(1, s0)
                pool.wait_ge(low_ready[Z], s0 + HALF + 1)
                copy_masks(0, s0 + BODY)
                pool.wait_ge(low_ready[Z], s0 + HALF + 2)
                copy_out(0, s0 + HALF)
            pool.wait_ge(low_ready[Z], NBODY * BODY + 1)
            copy_out(1, NBODY * BODY)

        def product(pe, out, weights, moving, start=False, stop=False):
            return pe.matmul(out, weights, moving, start=start, stop=stop, skip_group_check=True)

        TERMS = ((0, 0), (1, 0), (0, 1))

        def projections(pe, half, t0):
            n = HALF * NB
            work = []

            def add(c, g, weights, moving):
                first = not any(w[0] == c for w in work)
                work.append((c, lambda: product(pe, pz[c][half][:, :, g, :], weights, moving, start=first)))

            for c in CHAINS:
                base, size = (0, H0) if c < Z else (4 * H0, H1)
                for g, gate in enumerate(GATES):
                    col = gate * size + c % Z * P
                    add(c, g, bw[:, base + col:base + col + P], RHS[:, bass.ds((t0 + LAG * (c < Z)) * NB, n)])
                    for wp, mp in TERMS:
                        if c < Z:
                            add(c, g, w0[:, wp, 0, col:col + P], XN[:, mp, bass.ds(t0 * NB, n)])
                        else:
                            for k in range(2):
                                add(c, g, w1[:, wp, k, col:col + P],
                                    hist[:, k, mp, half * HALF:(half + 1) * HALF, :].rearrange("p t b -> p (t b)"))
            return [w[1] for w in work]

        @block.tensor
        def _(pe):
            pe.wait_ge(low_split, 5)
            pe.wait_ge(rows_in, 32)
            pe.wait_ge(state_zero, 1)
            for mm in projections(pe, 0, 0):
                mm()

            def step(j, s, project):
                half, jj = j // HALF, j % HALF
                old = (j - 2) % BODY

                def by(c, k, part, gates=range(4)):
                    for g in gates:
                        u, kk, col = (u1, 0, GATES[g] * H1) if c == Z else (u0, k, GATES[g] * H0 + c * P)
                        for wp in range(2 - part):
                            mm = product(pe, pz[c][half][:, jj, g, :], u[:, wp, kk, col:col + P],
                                         hist[:, k, part, old, :], stop=(part == 1 and k != X))
                    return mm

                HI, LO, FI, OG = 0, 1, (0, 1), (2, 3)
                pe.wait_ge(high_ready[X], s + 1)
                by(X, X, HI)
                by(Y, X, HI)
                pe.wait_ge(low_ready[X], s + 1)
                by(X, X, LO)
                pe.wait_ge(high_ready[Y], s + 1)
                by(X, Y, HI)
                pe.wait_ge(low_ready[Y], s + 1)
                by(X, Y, LO).then_inc(input_ready[X], 1)
                by(Y, X, LO)
                by(Y, Y, HI)
                by(Y, Y, LO).then_inc(input_ready[Y], 1)
                project()
                pe.wait_ge(high_ready[Z], s + 1)
                by(Z, Z, HI)
                pe.wait_ge(low_ready[Z], s + 1)
                by(Z, Z, LO).then_inc(input_ready[Z], 1)
                project()

            with pe.Fori(0, NBODY) as i:
                s0 = i * BODY
                for half in range(2):
                    work = projections(pe, 1 - half, s0 + (half + 1) * HALF)
                    for jj in range(HALF):
                        def project():
                            if jj >= 1 and work:
                                work.pop(0)()

                        step(half * HALF + jj, s0 + half * HALF + jj, project)
                    assert not work

        @block.scalar
        def _(act):
            def gates(c, j, s):
                z = pz[c][j // HALF][:, j % HALF, :, :]
                act.wait_ge(input_ready[c], s + 1)
                nc.scalar.activation(fio[c][:, :, :, 1], z[:, 0:3, :], ACT.Sigmoid, scale=1 / WSCALE)
                nc.scalar.activation(tg[c][:, :], z[:, 3, :], ACT.Tanh, scale=1 / WSCALE).then_inc(gates_ready[c], 1)

            def tanh(c, j, s):
                act.wait_ge(cell_ready[c], s + 1)
                nc.scalar.activation(tc[c][:, :], cig[c][:, (j + 1) % 2, 1::2], ACT.Tanh).then_inc(tanh_ready[c], 1)

            with act.Fori(0, NBODY) as i:
                for j in range(BODY):
                    s = i * BODY + j
                    gates(X, j, s)
                    gates(Y, j, s)
                    tanh(X, j, s)
                    gates(Z, j, s)
                    tanh(Y, j, s)
                    tanh(Z, j, s)

        @block.vector
        def _(dve):
            nc.vector.memset(hist[:, :, :, :, :], 0.0)
            nc.vector.memset(states[:, :, :], 0.0)
            for c in CHAINS:
                nc.vector.memset(cig[c][:, :, :], 0.0)
                nc.vector.memset(fio[c][:, :, :, :], 0.0)
                dve.sem_inc(high_ready[c], 1)
                dve.sem_inc(low_ready[c], 1)
                ins = nc.vector.memset(og[c][:, :], 0.0)
            ins.then_inc(state_zero, 1)
            dve.wait_ge(weights_in, 16 * 6)
            pairs = [(t[:, :, :], w[:, 0, :, :], w[:, 1, :, :]) for t, w in zip(full, (w0, u0, w1, u1))]
            pairs.append((biasf[:, :], bw[0:1, :], blow[:, :]))
            for f, hi, lo in pairs:
                nc.vector.tensor_scalar(hi, f, WSCALE, None, ALU.mult).then_inc(high_split, 1)
            dve.wait_ge(high_split, 5)
            for f, hi, lo in pairs:
                nc.vector.scalar_tensor_tensor(out=lo, in0=f, scalar=WSCALE, in1=hi, op0=ALU.mult, op1=ALU.subtract)\
                    .then_inc(low_split, 1)
            dve.wait_ge(state_zero, 1)

            def product_ig(c, j, s):
                dve.wait_ge(gates_ready[c], s + 1)
                nc.vector.tensor_tensor(cig[c][:, j % 2, 2::2], fio[c][:, 1, :, 1], tg[c][:, :], ALU.mult)\
                    .then_inc(product_ready[c], 1)

            def cell(c, j, s):
                dve.wait_ge(product_ready[c], s + 1)
                nc.vector.tensor_tensor_scan(out=cig[c][:, (j + 1) % 2, 0:2 * NB],
                                             data0=fio[c][:, 0, :, :].rearrange("p b k -> p (b k)"),
                                             data1=cig[c][:, j % 2, 1:], initial=0.0, op0=ALU.mult, op1=ALU.add)\
                    .then_inc(cell_ready[c], 1)

            def keep_o(c, j):
                nc.vector.copy_predicated(og[c][:, :], mask[:, c // Z, j, :], fio[c][:, 2, :, 1])

            def high(c, j, s):
                dve.wait_ge(tanh_ready[c], s + 1)
                nc.vector.tensor_tensor(hist[:, c, 0, (j - 1) % BODY, :], og[c][:, :], tc[c][:, :], ALU.mult)\
                    .then_inc(high_ready[c], 1)

            def whole(c, j):
                to = states[:, (j - 1) % BODY, :] if c == Z else new[c][:, :]
                nc.vector.tensor_tensor(to, og[c][:, :], tc[c][:, :], ALU.mult).then_inc(full_ready[c], 1)

            def low(c, j, s):
                at = (j - 1) % BODY
                dve.wait_ge(full_ready[c], s + 1)
                nc.vector.tensor_tensor(hist[:, c, 1, at, :], states[:, at, :] if c == Z else new[c][:, :],
                                        hist[:, c, 0, at, :], ALU.subtract).then_inc(low_ready[c], 1)

            with dve.Fori(0, NBODY) as i:
                for j in range(BODY):
                    s = i * BODY + j
                    if j % HALF == 0:
                        dve.wait_ge(mask_ready, i * 4 + 2 * (j // HALF) + 2)
                    if j % HALF == 1:
                        dve.wait_ge(lat_copied, i * 2 + j // HALF + 1)
                    product_ig(X, j, s)
                    cell(X, j, s)
                    keep_o(X, j)
                    product_ig(Y, j, s)
                    keep_o(Y, j)
                    cell(Y, j, s)
                    high(X, j, s)
                    whole(X, j)
                    product_ig(Z, j, s)
                    keep_o(Z, j)
                    low(X, j, s)
                    high(Y, j, s)
                    whole(Y, j)
                    cell(Z, j, s)
                    low(Y, j, s)
                    high(Z, j, s)
                    whole(Z, j)
                    low(Z, j, s)


def mixture(nc, tokens, ident, LAT, LAT0, ln_g, ln_b, wg_group, wg_inner, W1, b1, W2, b2, gln_g, gln_b, out, T, TP):
    G, E, _, FH = W1.shape
    HC = FH // P
    NTILE = TP // BODY
    NGATE = G + 1
    NEXP = G * E
    NHID = 4
    CH = 2
    NCH = 2 * NEXP // CH
    AHEAD = 2
    assert NTILE % 2 == 0 and NEXP % NHID == 0
    TERMS = ((0, 0), (1, 0), (0, 1))
    with ExitStack() as ctx:
        def sb(name, shape, dt=F32):
            return ctx.enter_context(nc.sbuf_tensor(name, shape, dt))

        def psum(name):
            return ctx.enter_context(nc.psum_tensor(name, [P, 512], F32))

        def sem(name):
            return ctx.enter_context(nc.semaphore(name))

        w1 = sb("w1e", [P, 2, NEXP, FH], F16)
        w2 = sb("w2e", [P, 2, NEXP, HC, P], F16)
        stage = sb("stage", [P, 2, CH * FH])
        b1r = sb("b1r", [NEXP * HC, P])
        b1c = sb("b1c", [P, NEXP, HC])
        b2s = sb("b2s", [E, G, P])
        wg = sb("wg", [P, G])
        wi = sb("wi", [P, G, E])
        vec = sb("vec", [P, 2 + 2 * G, P])
        iota = sb("iota", [P, NGATE, E])
        iotau = sb("iotau", [P, NGATE, E], U32)
        eps = sb("eps_e", [P, 1])
        ht = sb("ht", [P, P])
        latc = sb("latc", [P, P])
        h1 = sb("h1", [P, 2, P])
        xf = sb("xf", [P, 2, P])
        z = sb("z", [P, 2, P])
        zn = sb("zn", [P, P])
        zs = sb("zs", [P, P])
        xfT = sb("xfT", [P, P])
        zT = sb("zT", [P, P])
        zTp = sb("zTp", [P, 2, 2, P], F16)
        stats = sb("stats_e", [P, 6])
        mv = sb("mv_e", [P, 2])
        std = sb("std_e", [P, 1])
        rstd = sb("rstd_e", [P, 1])
        lg = sb("lg", [P, NGATE, E])
        top = sb("top", [P, NGATE, 8])
        ix = sb("ix", [P, NGATE, 8], U32)
        ixf = sb("ixf", [P, NGATE, 8])
        gap = sb("gap", [P, NGATE])
        p1 = sb("p1", [P, NGATE])
        p2 = sb("p2", [P, NGATE])
        m1 = sb("m1", [P, NGATE, E])
        m2 = sb("m2", [P, NGATE, E])
        wt = sb("wt", [P, 2, NGATE, E])
        wts = sb("wts", [P, 2, NGATE, E])
        wtT = sb("wtT", [E, 2, G, P])
        hid = sb("hid", [P, 2, HC, P])
        hidp = sb("hidp", [P, NHID, 2, HC, P], F16)
        moe = sb("moe", [P, 2, P])
        gstats = sb("gstats", [P, 6])
        gmv = sb("gmv", [P, 2])
        gstd = sb("gstd", [P, 1])
        grstd = sb("grstd", [P, 1])
        gn = sb("gn", [P, P])
        gs = sb("gs", [P, P])
        y = sb("y", [P, P])
        acc = sb("acc", [P, P])
        tmp = sb("tmp", [P, P])
        res = sb("res", [P, P])
        pH = [psum("pH0"), psum("pH1")]
        pO = [psum("pO0"), psum("pO1")]
        pA = psum("pA")
        pB = psum("pB")
        pL = psum("pL")
        pM = psum("pM")

        small_in = sem("small_in")
        chunk_in = [sem("chunk_in0"), sem("chunk_in1")]
        chunk_high = sem("chunk_high")
        chunk_low = sem("chunk_low")
        consts = sem("econsts")
        b1_turned = sem("b1_turned")
        b1_done = sem("b1_done")
        iota_done = sem("iota_done")
        tile_in = sem("etile_in")
        lat_cut = sem("lat_cut")
        lat_turned = sem("lat_turned")
        h1_done = sem("h1_done")
        stats_done = sem("estats_done")
        mv_done = sem("emv_done")
        std_done = sem("estd_done")
        rstd_done = sem("erstd_done")
        xf_done = sem("xf_done")
        zn_done = sem("zn_done")
        zs_done = sem("zs_done")
        z_done = sem("z_done")
        x_turned = sem("x_turned")
        xT_done = sem("xT_done")
        zlow_done = sem("zlow_done")
        logits = sem("logits")
        lg_done = sem("lg_done")
        top_done = sem("top_done")
        gap_done = sem("gap_done")
        ix_done = sem("ix_done")
        ixf_done = sem("ixf_done")
        p_done = sem("p_done")
        eq_done = sem("eq_done")
        share_done = sem("share_done")
        wt_done = sem("wt_done")
        wts_done = sem("wts_done")
        wt_turned = sem("wt_turned")
        wtT_done = sem("wtT_done")
        bias_ready = sem("bias_ready")
        moe_begun = sem("moe_begun")
        up_ready = sem("up_ready")
        hid_ready = sem("hid_ready")
        hid_high = [sem("hid_high_a"), sem("hid_high_v")]
        hid_low = sem("hid_low")
        down_ready = sem("down_ready")
        mixed = sem("mixed")
        gstats_done = sem("gstats_done")
        gmv_done = sem("gmv_done")
        gstd_done = sem("gstd_done")
        grstd_done = sem("grstd_done")
        gn_done = sem("gn_done")
        gs_done = sem("gs_done")
        y_done = sem("y_done")
        acc_done = sem("acc_done")
        acc_sum = sem("acc_sum")
        res_done = sem("res_done")
        res_out = sem("res_out")
        block = ctx.enter_context(nc.Block())
        NSMALL = 6 + 2 * G

        def bc(v):
            return v.rearrange("(a d) -> a d", a=1).to_broadcast([P, P])

        def parts(c, part):
            n = c % (NCH // 2) * CH
            if c < NCH // 2:
                return w1[:, part, n:n + CH, :].rearrange("p n h -> p (n h)")
            return w2[:, part, n:n + CH, :, :].rearrange("p n c d -> p (n c d)")

        @block.sync
        def _(sp):
            w1_in = W1.rearrange("g e d h -> d (g e) h")
            w2_in = W2.rearrange("g e (c p) d -> p (g e) c d", p=P)
            for c in range(NCH):
                if c >= 2:
                    sp.wait_ge(chunk_low, c - 1)
                n = c % (NCH // 2) * CH
                if c < NCH // 2:
                    sp.dma_start(stage[:, c % 2, :].rearrange("p (n h) -> p n h", h=FH), w1_in[:, n:n + CH, :])\
                        .then_inc(chunk_in[c % 2], 16)
                else:
                    sp.dma_start(stage[:, c % 2, :].rearrange("p (n c d) -> p n c d", c=HC, d=P),
                                 w2_in[:, n:n + CH, :, :]).then_inc(chunk_in[c % 2], 16)
                if c == 1:
                    sp.dma_start(b1r[:, :], b1.rearrange("g e (c p) -> (g e c) p", p=P)).then_inc(small_in, 16)
                    sp.dma_start(b2s[:, :, :], b2.rearrange("g e d -> e g d")).then_inc(small_in, 16)
                    sp.dma_start(wg[:, :], wg_group).then_inc(small_in, 16)
                    sp.dma_start(wi[:, :, :], wg_inner.rearrange("g d e -> d g e")).then_inc(small_in, 16)
                    sp.dma_start(vec[:, 0, :], bc(ln_g)).then_inc(small_in, 16)
                    sp.dma_start(vec[:, 1, :], bc(ln_b)).then_inc(small_in, 16)
                    for g in range(G):
                        sp.dma_start(vec[:, 2 + 2 * g, :], bc(gln_g[g])).then_inc(small_in, 16)
                        sp.dma_start(vec[:, 3 + 2 * g, :], bc(gln_b[g])).then_inc(small_in, 16)
            tiles = tokens.rearrange("(n t) b d -> n (t b) d", t=BODY)

            def load(t):
                sp.wait_ge(h1_done, t + 1)
                sp.dma_start(ht[:, :], tiles[bass.ds(t, 1)].rearrange("n p d -> (n p) d")).then_inc(tile_in, 16)

            def store(i, n):
                sp.wait_ge(res_done, i + 1)
                for b in range(NB):
                    sp.dma_start(out[b, bass.ds(i * BODY, n), :], res[b:n * NB:NB, :]).then_inc(res_out, 16)

            load(0)
            with sp.Fori(0, NTILE - 1) as i:
                load(i + 1)
                store(i, BODY)
            load(NTILE)
            store(NTILE - 1, T - (NTILE - 1) * BODY)
            sp.wait_ge(res_out, 16 * NB * (NTILE + 1))

        @block.gpsimd
        def _(pool):
            pool.iota(iotau[:, :, :], pattern=[[0, NGATE], [1, E]], base=0, channel_multiplier=0).then_inc(consts, 1)
            pool.memset(eps[:, :], EPS).then_inc(consts, 1)
            pool.memset(lg[:, 0, :], -3e38).then_inc(consts, 1)

        @block.tensor
        def _(pe):
            pe.wait_ge(small_in, 16 * NSMALL)
            pe.matmul(pA[:, 0:P], b1r[:, :], ident[:, :], start=True, stop=True).then_inc(b1_turned, 1)
            pe.wait_ge(b1_done, 1)

            def head(n, t, u):
                if n == 1:
                    pe.wait_ge(lat_cut, t + 1)
                    pe.transpose(pA[:, 0:P], latc[:, :], ident[:, :]).then_inc(lat_turned, 1)
                if n == 16:
                    pe.wait_ge(z_done, t + 1)
                    pe.transpose(pA[:, 0:P], xf[:, u, :], ident[:, :])
                    pe.transpose(pB[:, 0:P], z[:, u, :], ident[:, :]).then_inc(x_turned, 1)
                if n == 19:
                    pe.wait_ge(xT_done, t + 1)
                    pe.matmul(pL[:, 0:G], xfT[:, :], wg[:, :], start=True, stop=True)
                    pe.matmul(pL[:, E:E + G * E], zT[:, :], wi[:, :, :].rearrange("p g e -> p (g e)"), start=True,
                              stop=True).then_inc(logits, 1)
                if n == 28:
                    pe.wait_ge(wt_done, t + 1)
                    for g in range(G):
                        mm = pe.matmul(pB[0:E, g * P:(g + 1) * P], wt[:, u, 1 + g, :], ident[:, :], start=True,
                                       stop=True)
                    mm.then_inc(wt_turned, 1)

            def up(t, u, n):
                m = t * NEXP + n
                if n == 0:
                    pe.wait_ge(zlow_done, t + 1)
                pe.wait_ge(hid_ready, freed(m))
                for c in range(HC):
                    for wp, zp in TERMS:
                        mm = pe.matmul(pH[n % 2][:, c * P:(c + 1) * P], w1[:, wp, n, c * P:(c + 1) * P],
                                       zTp[:, u, zp, :], start=(wp + zp == 0), stop=(zp == 1))
                mm.then_inc(up_ready, 1)

            def down(t, n):
                m = t * NEXP + n
                pe.wait_ge(mixed, freed(m))
                pe.wait_ge(hid_low, done(m))
                for c in range(HC):
                    for wp, hp in TERMS:
                        mm = pe.matmul(pO[n % 2][:, 0:P], hidp[:, n % NHID, hp, c, :], w2[:, wp, n, c, :],
                                       start=(c + wp + hp == 0), stop=(c == HC - 1 and hp == 1))
                mm.then_inc(down_ready, 1)

            for n in range(NEXP):
                head(n, 0, 0)
            pe.wait_ge(chunk_low, NCH)
            for n in range(AHEAD):
                up(0, 0, n)
            with pe.Fori(0, NTILE // 2) as pair:
                for u in range(2):
                    i = 2 * pair + u
                    for n in range(NEXP):
                        head(n, i + 1, 1 - u)
                        if n == 0:
                            pe.wait_ge(wtT_done, i + 1)
                        if n % E == 0:
                            pe.wait_ge(moe_begun, i * G + n // E + 1)
                            pe.matmul(pM[:, 0:P], wtT[:, u, n // E, :], b2s[:, n // E, :], start=True, stop=True)\
                                .then_inc(bias_ready, 1)
                        if n + AHEAD < NEXP:
                            up(i, u, n + AHEAD)
                        else:
                            up(i + 1, 1 - u, n + AHEAD - NEXP)
                        down(i, n)

        @block.scalar
        def _(act):
            for c in range(NCH):
                act.wait_ge(chunk_in[c % 2], 16 * (c // 2 + 1))
                nc.scalar.activation(parts(c, 0), stage[:, c % 2, :], ACT.Copy, scale=FSCALE).then_inc(chunk_high, 1)
            act.wait_ge(b1_turned, 1)
            nc.scalar.activation(b1c[:, :, :].rearrange("p n c -> p (n c)"), pA[:, 0:P], ACT.Copy, scale=FSCALE)\
                .then_inc(b1_done, 1)
            act.wait_ge(consts, 3)

            def head(n, t, u):
                if n == 0:
                    nc.scalar.copy(latc[:, :], LAT[:, bass.ds((t * BODY + LAT0) * NB, NT)]).then_inc(lat_cut, 1)
                if n in (5, 10):
                    act.wait_ge(mv_done, t * 2 + n // 5)
                    nc.scalar.activation(std[:, :], mv[:, 1:2], ACT.Sqrt, bias=eps[:, :]).then_inc(std_done, 1)
                if n == 17:
                    act.wait_ge(x_turned, t + 1)
                    nc.scalar.copy(xfT[:, :], pA[:, 0:P])
                    nc.scalar.copy(zT[:, :], pB[:, 0:P])
                    nc.scalar.copy(zTp[:, u, 0, :], pB[:, 0:P]).then_inc(xT_done, 1)
                if n == 23:
                    act.wait_ge(gap_done, t + 1)
                    nc.scalar.activation(p1[:, :], gap[:, :], ACT.Sigmoid)
                    nc.scalar.activation(p2[:, :], gap[:, :], ACT.Sigmoid, scale=-1.0).then_inc(p_done, 1)
                if n == 29:
                    act.wait_ge(wt_turned, t + 1)
                    nc.scalar.copy(wtT[:, u, :, :].rearrange("p g n -> p (g n)"), pB[0:E, 0:G * P])\
                        .then_inc(wtT_done, 1)

            def end(i, g):
                act.wait_ge(gmv_done, i * G + g + 1)
                nc.scalar.activation(gstd[:, :], gmv[:, 1:2], ACT.Sqrt, bias=eps[:, :]).then_inc(gstd_done, 1)

            def hidden(t, n):
                m = t * NEXP + n
                act.wait_ge(hid_low, freed(m))
                act.wait_ge(up_ready, m + 1)
                for c in range(HC):
                    ins = nc.scalar.activation(hid[:, n % 2, c, :], pH[n % 2][:, c * P:(c + 1) * P], ACT.Relu,
                                               bias=b1c[:, n, c:c + 1])
                ins.then_inc(hid_ready, 1)
                if n % 2 == 0:
                    act.wait_ge(hid_ready, done(m))
                    nc.scalar.copy(hidp[:, n % NHID, 0, :, :], hid[:, 0, :, :]).then_inc(hid_high[0], 1)

            for n in range(NEXP):
                head(n, 0, 0)
            for n in range(AHEAD):
                hidden(0, n)
            with act.Fori(0, NTILE // 2) as pair:
                for u in range(2):
                    i = 2 * pair + u
                    for n in range(NEXP):
                        if n + AHEAD < NEXP:
                            hidden(i, n + AHEAD)
                        else:
                            hidden(i + 1, n + AHEAD - NEXP)
                        head(n, i + 1, 1 - u)
                        if n % E == 2 and n > E:
                            end(i, n // E - 1)
                    end(i, G - 1)

        @block.vector
        def _(dve):
            dve.sem_inc(h1_done, 1)
            dve.sem_inc(hid_ready, TOKENS)
            dve.sem_inc(hid_low, TOKENS)
            dve.sem_inc(mixed, TOKENS)
            dve.sem_inc(moe_begun, 1)
            dve.sem_inc(acc_done, 1)
            dve.sem_inc(res_out, 16 * NB)
            for c in range(NCH):
                dve.wait_ge(chunk_high, c + 1)
                nc.vector.scalar_tensor_tensor(out=parts(c, 1), in0=stage[:, c % 2, :], scalar=FSCALE,
                                               in1=parts(c, 0), op0=ALU.mult, op1=ALU.subtract).then_inc(chunk_low, 1)
            dve.wait_ge(consts, 3)
            nc.vector.tensor_copy(iota[:, :, :], iotau[:, :, :]).then_inc(iota_done, 1)
            dve.wait_ge(iota_done, 1)
            dve.wait_ge(small_in, 16 * NSMALL)

            def wide(a):
                return a.rearrange("p (g a) -> p g a", a=1).to_broadcast([P, NGATE, E])

            def norm(n, k, to, src):
                if k == 0:
                    return nc.vector.bn_stats(stats[:, :], src).then_inc(stats_done, 1)
                if k == 1:
                    dve.wait_ge(stats_done, n + 1)
                    nc.vector.memset(rstd[:, :], 0.0)
                    return nc.vector.bn_aggr(mv[:, :], stats[:, :]).then_inc(mv_done, 1)
                if k == 2:
                    dve.wait_ge(std_done, n + 1)
                    return nc.vector.reciprocal(rstd[:, :], std[:, :]).then_inc(rstd_done, 1)
                dve.wait_ge(rstd_done, n + 1)
                return nc.vector.tensor_scalar(to, src, mv[:, 0:1], rstd[:, :], ALU.subtract, ALU.mult)

            def head(n, t, u):
                if n == 2:
                    dve.wait_ge(tile_in, 16 * t + 16)
                    dve.wait_ge(lat_turned, t + 1)
                    nc.vector.tensor_tensor(h1[:, u, :], ht[:, :], pA[:, 0:P], ALU.add).then_inc(h1_done, 1)
                if n == 3:
                    dve.wait_ge(h1_done, t + 2)
                    norm(t * 2, 0, None, h1[:, u, :])
                if n == 4:
                    norm(t * 2, 1, None, None)
                if n == 6:
                    norm(t * 2, 2, None, None)
                if n == 7:
                    norm(t * 2, 3, xf[:, u, :], h1[:, u, :]).then_inc(xf_done, 1)
                if n == 8:
                    dve.wait_ge(xf_done, t + 1)
                    norm(t * 2 + 1, 0, None, xf[:, u, :])
                if n == 9:
                    norm(t * 2 + 1, 1, None, None)
                if n == 11:
                    norm(t * 2 + 1, 2, None, None)
                if n == 12:
                    norm(t * 2 + 1, 3, zn[:, :], xf[:, u, :]).then_inc(zn_done, 1)
                if n == 13:
                    dve.wait_ge(zn_done, t + 1)
                    nc.vector.tensor_tensor(zs[:, :], zn[:, :], vec[:, 0, :], ALU.mult).then_inc(zs_done, 1)
                if n == 14:
                    dve.wait_ge(zs_done, t + 1)
                    nc.vector.tensor_tensor(z[:, u, :], zs[:, :], vec[:, 1, :], ALU.add).then_inc(z_done, 1)
                if n == 18:
                    dve.wait_ge(xT_done, t + 1)
                    nc.vector.tensor_tensor(zTp[:, u, 1, :], zT[:, :], zTp[:, u, 0, :], ALU.subtract)\
                        .then_inc(zlow_done, 1)
                if n == 20:
                    dve.wait_ge(logits, t + 1)
                    nc.vector.tensor_copy(lg[:, 0, 0:G], pL[:, 0:G])
                    nc.vector.tensor_copy(lg[:, 1:, :].rearrange("p g e -> p (g e)"), pL[:, E:E + G * E])\
                        .then_inc(lg_done, 1)
                if n == 21:
                    dve.wait_ge(lg_done, t + 1)
                    nc.vector.memset(gap[:, :], 0.0)
                    for g in range(NGATE):
                        ins = nc.vector.max(top[:, g, :], lg[:, g, :])
                    ins.then_inc(top_done, 1)
                if n == 22:
                    dve.wait_ge(top_done, t + 1)
                    nc.vector.tensor_tensor(gap[:, :], top[:, :, 0], top[:, :, 1], ALU.subtract).then_inc(gap_done, 1)
                    for g in range(NGATE):
                        ins = nc.vector.max_index(ix[:, g, :], top[:, g, :], lg[:, g, :])
                    ins.then_inc(ix_done, 1)
                if n == 23:
                    dve.wait_ge(ix_done, t + 1)
                    nc.vector.tensor_copy(ixf[:, :, :], ix[:, :, :]).then_inc(ixf_done, 1)
                if n == 24:
                    dve.wait_ge(ixf_done, t + 1)
                    nc.vector.tensor_tensor(m1[:, :, :], iota[:, :, :], wide(ixf[:, :, 0]), ALU.is_equal)
                    nc.vector.tensor_tensor(m2[:, :, :], iota[:, :, :], wide(ixf[:, :, 1]), ALU.is_equal)\
                        .then_inc(eq_done, 1)
                if n == 25:
                    dve.wait_ge(p_done, t + 1)
                    dve.wait_ge(eq_done, t + 1)
                    nc.vector.tensor_tensor(m1[:, :, :], m1[:, :, :], wide(p1[:, :]), ALU.mult)
                    nc.vector.tensor_tensor(m2[:, :, :], m2[:, :, :], wide(p2[:, :]), ALU.mult).then_inc(share_done, 1)
                if n == 26:
                    dve.wait_ge(share_done, t + 1)
                    nc.vector.tensor_tensor(wt[:, u, :, :], m1[:, :, :], m2[:, :, :], ALU.add).then_inc(wt_done, 1)
                if n == 27:
                    dve.wait_ge(wt_done, t + 1)
                    nc.vector.tensor_scalar(wts[:, u, :, :], wt[:, u, :, :], 1 / (FSCALE * FSCALE), None, ALU.mult)\
                        .then_inc(wts_done, 1)

            def end(k, i, u, g):
                n, m = i * G + g, moe[:, g % 2, :]
                if k == 0:
                    dve.wait_ge(mixed, done(i * NEXP + g * E + E - 1))
                    nc.vector.bn_stats(gstats[:, :], m).then_inc(gstats_done, 1)
                if k == 1:
                    dve.wait_ge(gstats_done, n + 1)
                    nc.vector.memset(grstd[:, :], 0.0)
                    nc.vector.bn_aggr(gmv[:, :], gstats[:, :]).then_inc(gmv_done, 1)
                if k == 2:
                    dve.wait_ge(gstd_done, n + 1)
                    nc.vector.reciprocal(grstd[:, :], gstd[:, :]).then_inc(grstd_done, 1)
                if k == 3:
                    dve.wait_ge(grstd_done, n + 1)
                    nc.vector.tensor_scalar(gn[:, :], m, gmv[:, 0:1], grstd[:, :], ALU.subtract, ALU.mult)\
                        .then_inc(gn_done, 1)
                if k == 4:
                    dve.wait_ge(gn_done, n + 1)
                    nc.vector.tensor_tensor(gs[:, :], gn[:, :], vec[:, 2 + 2 * g, :], ALU.mult).then_inc(gs_done, 1)
                if k == 5:
                    dve.wait_ge(gs_done, n + 1)
                    nc.vector.tensor_tensor(y[:, :], gs[:, :], vec[:, 3 + 2 * g, :], ALU.add).then_inc(y_done, 1)
                if k == 6:
                    dve.wait_ge(y_done, n + 1)
                    dve.wait_ge(acc_done, n + 1)
                    if g == 0:
                        nc.vector.tensor_scalar(acc[:, :], y[:, :], wt[:, u, 0, g:g + 1], None, ALU.mult)\
                            .then_inc(acc_done, 1)
                    else:
                        nc.vector.scalar_tensor_tensor(out=acc[:, :], in0=y[:, :], scalar=wt[:, u, 0, g:g + 1],
                                                       in1=acc[:, :], op0=ALU.mult, op1=ALU.add).then_inc(acc_done, 1)

            def high(t, n):
                if n % 2 == 1:
                    dve.wait_ge(hid_ready, done(t * NEXP + n))
                    nc.vector.tensor_copy(hidp[:, n % NHID, 0, :, :], hid[:, 1, :, :]).then_inc(hid_high[1], 1)

            def low(t, n):
                dve.wait_ge(hid_high[n % 2], t * (NEXP // 2) + n // 2 + 1)
                nc.vector.tensor_tensor(hidp[:, n % NHID, 1, :, :], hid[:, n % 2, :, :], hidp[:, n % NHID, 0, :, :],
                                        ALU.subtract).then_inc(hid_low, 1)

            def mix(i, u, n):
                m = i * NEXP + n
                to = moe[:, n // E % 2, :]
                if n % E == 0:
                    dve.wait_ge(moe_begun, i * G + n // E + 2)
                dve.wait_ge(mixed, freed(m + 1))
                dve.wait_ge(down_ready, m + 1)
                nc.vector.scalar_tensor_tensor(out=to, in0=pO[n % 2][:, 0:P],
                                               scalar=wts[:, u, 1 + n // E, n % E:n % E + 1], in1=to,
                                               op0=ALU.mult, op1=ALU.add).then_inc(mixed, 1)

            for n in range(NEXP):
                head(n, 0, 0)
            for n in range(AHEAD):
                high(0, n)
                low(0, n)
            with dve.Fori(0, NTILE // 2) as pair:
                for u in range(2):
                    i = 2 * pair + u
                    for n in range(NEXP):
                        t, nn = (i, n + AHEAD) if n + AHEAD < NEXP else (i + 1, n + AHEAD - NEXP)
                        if n % E == 0:
                            g = n // E
                            dve.wait_ge(wts_done, i + 1)
                            dve.wait_ge(bias_ready, i * G + g + 1)
                            nc.vector.tensor_tensor(moe[:, g % 2, :], z[:, u, :], pM[:, 0:P], ALU.add)\
                                .then_inc(moe_begun, 1)
                        high(t, nn)
                        head(n, i + 1, 1 - u)
                        mix(i, u, n)
                        low(t, nn)
                        if n >= E:
                            k = n % E
                            if k != 2:
                                end(k - (k > 2), i, u, n // E - 1)
                    for k in range(7):
                        end(k, i, u, G - 1)
                    dve.wait_ge(acc_done, i * G + G + 1)
                    nc.vector.tensor_tensor(tmp[:, :], acc[:, :], xf[:, u, :], ALU.add).then_inc(acc_sum, 1)
                    dve.wait_ge(acc_sum, i + 1)
                    dve.wait_ge(res_out, 16 * NB * (i + 1))
                    nc.vector.tensor_tensor(res[:, :], tmp[:, :], h1[:, u, :], ALU.add).then_inc(res_done, 1)


def fusion_kernel(nc, x, txt, tok_W, tok_b, tok_cls, W0, U0, b0, W1, U1, b1, ln_g, ln_b, wg_group, wg_inner,
                  fW1, fb1, fW2, fb2, gln_g, gln_b, out):
    T = 1 + (x.shape[2] // 4) * (x.shape[3] // 4) + txt.shape[1]
    assert x.shape[0] == NB and txt.shape[2] == P and (T + LAG) % BODY == 0
    NBODY = (T + LAG) // BODY
    TP = NBODY * BODY
    TX = TP + HALF
    LAT0 = LAG - 1 + HALF
    tokens = nc.dram_tensor("tokens", [TP + BODY, NB, P], F32, kind="Internal").ap()
    with ExitStack() as ctx:
        def sb(name, shape, dt=F32):
            return ctx.enter_context(nc.sbuf_tensor(name, shape, dt))

        ident = sb("ident", [P, P])
        LAT = sb("LAT", [P, (TP + BODY + LAT0) * NB])
        with ExitStack() as inner:
            XN = inner.enter_context(nc.sbuf_tensor("XN", [P, 2, TX * NB], F16))
            CNT = inner.enter_context(nc.sbuf_tensor("CNT", [P, (LAG + TX) * NB], U16))
            RHS = inner.enter_context(nc.sbuf_tensor("RHS", [3, (LAG + TX) * NB], F16))
            make_tokens(nc, tokens, ident, XN, CNT, RHS, x, txt, tok_W, tok_b, tok_cls, T, TP)
            recur(nc, XN, CNT, RHS, LAT, W0, U0, b0, W1, U1, b1, NBODY)
        mixture(nc, tokens, ident, LAT, LAT0, ln_g, ln_b, wg_group, wg_inner, fW1, fb1, fW2, fb2, gln_g, gln_b,
                out, T, TP)


_INS = ['x', 'txt', 'L0_tok_W', 'L0_tok_b', 'L0_tok_cls', 'L0_attn_W0', 'L0_attn_U0', 'L0_attn_b0', 'L0_attn_W1',
        'L0_attn_U1', 'L0_attn_b1', 'L0_ffn_ln_g', 'L0_ffn_ln_b', 'L0_ffn_wg_group', 'L0_ffn_wg_inner', 'L0_ffn_W1',
        'L0_ffn_b1', 'L0_ffn_W2', 'L0_ffn_b2', 'L0_ffn_gln_g', 'L0_ffn_gln_b']


def kernel(**inputs):
    import numpy as _np
    import concourse.bacc as _bacc
    from concourse import mybir as _mybir
    from concourse.bass_utils import run_bass_kernel_spmd as _run

    nc = _bacc.Bacc("TRN2", target_bir_lowering=False, num_devices=1)
    arrays, args = {}, []
    for name in _INS:
        a = _np.ascontiguousarray(inputs[name])
        arrays[f"in_{name}_dram"] = a
        args.append(nc.dram_tensor(f"in_{name}_dram", a.shape, _mybir.dt.from_np(a.dtype), kind="ExternalInput").ap())
    x, txt = inputs['x'], inputs['txt']
    shape = (x.shape[0], 1 + (x.shape[2] // 4) * (x.shape[3] // 4) + txt.shape[1], txt.shape[2])
    out = nc.dram_tensor("out_0_dram", shape, _mybir.dt.float32, kind="ExternalOutput").ap()
    fusion_kernel(nc, *args, out)
    r = _run(nc, [arrays], core_ids=[0])
    return r.results[0]["out_0_dram"]
```

```python
from contextlib import ExitStack

import concourse.bass as bass
from concourse import mybir

ALU = mybir.AluOpType
ACT = mybir.ActivationFunctionType
F32 = mybir.dt.float32
F16 = mybir.dt.float16
BF16 = mybir.dt.bfloat16
U16 = mybir.dt.uint16
U32 = mybir.dt.uint32

P = 128
NB = 2
EPS = 1e-5
SAT = 32768.0
WSCALE = 64.0
FSCALE = 16.0
BODY = 64
HALF = BODY // 2
LAG = BODY - 1
NT = NB * BODY
GATES = (1, 0, 3, 2)
X, Y, Z = range(3)


TOKENS = 2


def done(n):
    return n + 1 + TOKENS


def freed(n):
    return n + 1


def make_tokens(nc, tokens, ident, XN, CNT, RHS, x, txt, tok_W, tok_b, tok_cls, T, TP):
    C, IH, IW = x.shape[1:]
    PS = 4
    GI, GJ = IH // PS, IW // PS
    KP = C * PS * PS
    NR = NB * GI
    NTILE = TP // BODY
    assert GJ % 2 == 0 and NTILE % 2 == 0
    with ExitStack() as ctx:
        def sb(name, shape, dt=F32):
            return ctx.enter_context(nc.sbuf_tensor(name, shape, dt))

        def psum(name):
            return ctx.enter_context(nc.psum_tensor(name, [P, 512], F32))

        def sem(name):
            return ctx.enter_context(nc.semaphore(name))

        img = sb("img", [NR, C * PS, IW])
        wtok = sb("wtok", [P, KP])
        wtokT = sb("wtokT", [KP, P])
        btok = sb("btok", [NR, P])
        patch = sb("patch", [NR, 2, KP])
        patchT = sb("patchT", [KP, 2, NR])
        emb = sb("emb", [NR, 2, P])
        zrow = sb("zrow", [NT, P])
        tile = sb("tile", [P, 2, P])
        xn = sb("xn", [P, 2, P])
        stats = sb("stats", [P, 2, 6])
        mv = sb("mv", [P, 2, 2])
        std = sb("std", [P, 2])
        rstd = sb("rstd", [P, 2])
        eps = sb("eps", [P, 1])
        ones = sb("ones", [P, P], BF16)
        live = sb("live", [P, 2, P], BF16)
        dead = sb("dead", [1, RHS.shape[1]], F16)
        pT = [psum("pT0"), psum("pT1")]
        pE = [psum("pE0"), psum("pE1")]
        pX = [psum("pX0"), psum("pX1")]
        pC = [psum("pC0"), psum("pC1")]

        inputs_in = sem("inputs_in")
        consts_done = sem("consts_done")
        ident_done = sem("ident_done")
        pads_done = sem("pads_done")
        rest_out = sem("rest_out")
        patch_cut = sem("patch_cut")
        patch_turned = sem("patch_turned")
        patchT_done = sem("patchT_done")
        emb_made = sem("emb_made")
        emb_done = sem("emb_done")
        emb_out = [sem("emb_out0"), sem("emb_out1")]
        wtok_turned = sem("wtok_turned")
        wtokT_done = sem("wtokT_done")
        tile_in = [sem("tile_in0"), sem("tile_in1")]
        stats_done = sem("stats_done")
        mv_done = sem("mv_done")
        std_done = sem("std_done")
        rstd_done = sem("rstd_done")
        xn_done = sem("xn_done")
        xn_turned = sem("xn_turned")
        xnt_done = sem("xnt_done")
        low_done = sem("low_done")
        counted = sem("counted")
        dead_done = sem("dead_done")
        dead_out = sem("dead_out")
        block = ctx.enter_context(nc.Block())

        emb_rows = tokens[1:1 + GI * GJ, :, :].rearrange("(i j) b d -> b i j d", j=GJ)
        tiles = tokens.rearrange("(n t) b d -> n (t b) d", t=BODY)

        @block.sync
        def _(sp):
            for b in range(NB):
                for c in range(C):
                    sp.dma_start(img[b * GI:(b + 1) * GI, c * PS:(c + 1) * PS, :],
                                 x[b, c].rearrange("(i p) w -> i p w", p=PS)).then_inc(inputs_in, 16)
            sp.dma_start(wtok[:, :], tok_W).then_inc(inputs_in, 16)
            sp.dma_start(btok[:, :], tok_b.rearrange("(a d) -> a d", a=1).to_broadcast([NR, P]))\
                .then_inc(inputs_in, 16)
            for b in range(NB):
                sp.dma_start(tokens[1 + GI * GJ:T, b, :], txt[b]).then_inc(rest_out, 16)
                sp.dma_start(tokens[0:1, b, :], tok_cls[0]).then_inc(rest_out, 16)
            sp.wait_ge(consts_done, 3)
            sp.dma_start(tokens[T:TP].rearrange("t b d -> (t b) d"), zrow[0:(TP - T) * NB, :]).then_inc(rest_out, 16)
            sp.dma_start(tokens[TP:TP + BODY].rearrange("t b d -> (t b) d"), zrow[:, :]).then_inc(rest_out, 16)
            with sp.Fori(0, GJ // 2) as pair:
                j = 2 * pair
                for u in range(2):
                    sp.wait_ge(emb_done, done(j + u))
                    for b in range(NB):
                        sp.dma_start(emb_rows[b, :, bass.ds(j + u, 1), :].rearrange("i a d -> i (a d)"),
                                     emb[b * GI:(b + 1) * GI, u, :]).then_inc(emb_out[u], 16)
            sp.wait_ge(rest_out, 16 * (2 * NB + 2))
            for u in range(2):
                sp.wait_ge(emb_out[u], 16 * NB * (GJ // 2 + 1))
            with sp.Fori(0, NTILE // 2) as pair:
                i = 2 * pair
                for u in range(2):
                    sp.wait_ge(xn_done, freed(i + u))
                    sp.dma_start(tile[:, u, :], tiles[bass.ds(i + u, 1)].rearrange("n p d -> (n p) d"))\
                        .then_inc(tile_in[u], 16)
            sp.wait_ge(dead_done, NTILE + TOKENS)
            sp.wait_ge(pads_done, 6)
            sp.dma_start(RHS[2:3, :], dead[:, :]).then_inc(dead_out, 16)
            sp.wait_ge(dead_out, 16)

        @block.gpsimd
        def _(pool):
            pool.memset(zrow[:, :], 0.0).then_inc(consts_done, 1)
            pool.memset(eps[:, :], EPS).then_inc(consts_done, 1)
            pool.memset(ones[:, :], 1.0).then_inc(consts_done, 1)
            pool.memset(ident[:, :], 0.0).then_inc(ident_done, 1)
            pool.wait_ge(ident_done, 1)
            pool.affine_select(out=ident[:, :], in_=ident[:, :], compare_op=ALU.not_equal, fill=1.0, base=0,
                               pattern=[[-1, P]], channel_multiplier=1).then_inc(ident_done, 1)
            pool.memset(CNT[:, 0:LAG * NB], 0.0).then_inc(pads_done, 1)
            pool.memset(CNT[:, (LAG + TP) * NB:], 0.0).then_inc(pads_done, 1)
            pool.memset(dead[:, 0:LAG * NB], WSCALE).then_inc(pads_done, 1)
            pool.memset(dead[:, (LAG + TP) * NB:], WSCALE).then_inc(pads_done, 1)
            pool.memset(XN[:, :, TP * NB:], 0.0).then_inc(pads_done, 1)
            pool.memset(RHS[0:2, :], 1.0).then_inc(pads_done, 1)

        @block.tensor
        def _(pe):
            pe.sem_inc(patch_turned, TOKENS)
            pe.sem_inc(emb_made, TOKENS)
            pe.sem_inc(xn_turned, TOKENS)
            pe.sem_inc(counted, TOKENS)
            pe.wait_ge(ident_done, 2)
            pe.wait_ge(inputs_in, 16 * (NB * C + 2))
            pe.transpose(pE[0][0:KP, 0:P], wtok[:, :], ident[:, :]).then_inc(wtok_turned, 1)
            pe.wait_ge(wtokT_done, 1)
            with pe.Fori(0, GJ // 2) as pair:
                j = 2 * pair
                for u in range(2):
                    pe.wait_ge(patch_cut, j + u + 1)
                    pe.wait_ge(patchT_done, freed(j + u))
                    pe.matmul(pT[u][0:KP, 0:NR], patch[:, u, :], ident[0:NR, 0:NR], start=True, stop=True)\
                        .then_inc(patch_turned, 1)
                for u in range(2):
                    pe.wait_ge(patchT_done, done(j + u))
                    pe.wait_ge(emb_done, freed(j + u))
                    pe.matmul(pE[u][0:NR, 0:P], patchT[:, u, :], wtokT[:, :], start=True, stop=True)\
                        .then_inc(emb_made, 1)
            with pe.Fori(0, NTILE // 2) as pair:
                i = 2 * pair
                for u in range(2):
                    pe.wait_ge(xn_done, done(i + u))
                    pe.wait_ge(low_done, freed(i + u))
                    pe.transpose(pX[u][:, 0:P], xn[:, u, :], ident[:, :]).then_inc(xn_turned, 1)
                for u in range(2):
                    pe.wait_ge(low_done, done(i + u))
                    pe.wait_ge(dead_done, freed(i + u))
                    pe.matmul(pC[u][:, 0:P], ones[:, :], live[:, u, :], start=True, stop=True).then_inc(counted, 1)

        @block.scalar
        def _(act):
            act.sem_inc(patchT_done, TOKENS)
            act.sem_inc(xnt_done, TOKENS)
            act.wait_ge(wtok_turned, 1)
            nc.scalar.copy(wtokT[:, :], pE[0][0:KP, 0:P]).then_inc(wtokT_done, 1)
            with act.Fori(0, GJ // 2) as pair:
                j = 2 * pair
                for u in range(2):
                    act.wait_ge(patch_turned, done(j + u))
                    act.wait_ge(emb_made, freed(j + u))
                    nc.scalar.copy(patchT[:, u, :], pT[u][0:KP, 0:NR]).then_inc(patchT_done, 1)
            act.wait_ge(consts_done, 3)
            with act.Fori(0, NTILE // 2) as pair:
                i = 2 * pair
                for u in range(2):
                    act.wait_ge(mv_done, i + u + 1)
                    nc.scalar.activation(std[:, u:u + 1], mv[:, u, 1:2], ACT.Sqrt, bias=eps[:, :])\
                        .then_inc(std_done, 1)
                for u in range(2):
                    act.wait_ge(xn_turned, done(i + u))
                    nc.scalar.copy(XN[:, 0, bass.ds((i + u) * NT, NT)], pX[u][:, 0:P]).then_inc(xnt_done, 1)

        @block.vector
        def _(dve):
            dve.sem_inc(emb_done, TOKENS)
            dve.sem_inc(xn_done, TOKENS)
            dve.sem_inc(dead_done, TOKENS)
            dve.sem_inc(low_done, TOKENS)
            for u in range(2):
                dve.sem_inc(emb_out[u], NB * 16)
            dve.wait_ge(inputs_in, 16 * (NB * C + 2))
            with dve.Fori(0, GJ // 2) as pair:
                j = 2 * pair
                for u in range(2):
                    dve.wait_ge(patch_turned, freed(j + u))
                    nc.vector.tensor_copy(patch[:, u, :].rearrange("p (r w) -> p r w", w=PS),
                                          img[:, :, bass.ds((j + u) * PS, PS)]).then_inc(patch_cut, 1)
                for u in range(2):
                    dve.wait_ge(emb_made, done(j + u))
                    dve.wait_ge(emb_out[u], NB * 16 * (pair + 1))
                    nc.vector.tensor_tensor(emb[:, u, :], pE[u][0:NR, 0:P], btok[:, :], ALU.add)\
                        .then_inc(emb_done, 1)
            dve.wait_ge(consts_done, 3)
            with dve.Fori(0, NTILE // 2) as pair:
                i = 2 * pair
                for u in range(2):
                    dve.wait_ge(tile_in[u], 8 * i + 16)
                    nc.vector.bn_stats(stats[:, u, :], tile[:, u, :]).then_inc(stats_done, 1)
                for u in range(2):
                    dve.wait_ge(stats_done, i + u + 1)
                    nc.vector.memset(rstd[:, u:u + 1], 0.0)
                    nc.vector.bn_aggr(mv[:, u, :], stats[:, u, :]).then_inc(mv_done, 1)
                for u in range(2):
                    dve.wait_ge(std_done, i + u + 1)
                    nc.vector.reciprocal(rstd[:, u:u + 1], std[:, u:u + 1]).then_inc(rstd_done, 1)
                for u in range(2):
                    dve.wait_ge(rstd_done, i + u + 1)
                    dve.wait_ge(xn_turned, freed(i + u))
                    nc.vector.tensor_scalar(xn[:, u, :], tile[:, u, :], mv[:, u, 0:1], rstd[:, u:u + 1],
                                            ALU.subtract, ALU.mult).then_inc(xn_done, 1)
                for u in range(2):
                    dve.wait_ge(xnt_done, done(i + u))
                    dve.wait_ge(counted, freed(i + u))
                    nc.vector.tensor_scalar(live[:, u, :], pX[u][:, 0:P], 0.0, None, ALU.not_equal)
                    nc.vector.tensor_tensor(XN[:, 1, bass.ds((i + u) * NT, NT)], pX[u][:, 0:P],
                                            XN[:, 0, bass.ds((i + u) * NT, NT)], ALU.subtract).then_inc(low_done, 1)
                for u in range(2):
                    dve.wait_ge(counted, done(i + u))
                    nc.vector.tensor_copy(CNT[:, bass.ds((i + u) * NT + LAG * NB, NT)], pC[u][:, 0:P])
                    nc.vector.tensor_scalar(dead[:, bass.ds((i + u) * NT + LAG * NB, NT)], pC[u][0:1, 0:P], 0.0, WSCALE,
                                            ALU.is_equal, ALU.mult).then_inc(dead_done, 1)


def recur(nc, XN, CNT, RHS, LAT, W0, U0, b0, W1, U1, b1, NBODY):
    H0, H1 = U0.shape[0], U1.shape[0]
    NCOL = 4 * (H0 + H1)
    assert H0 == 2 * P and H1 == P
    CHAINS = (X, Y, Z)
    with ExitStack() as ctx:
        def sb(name, shape, dt=F32):
            return ctx.enter_context(nc.sbuf_tensor(name, shape, dt))

        def sem(name):
            return ctx.enter_context(nc.semaphore(name))

        def each(make, name):
            return [make(f"{name}{c}") for c in "XYZ"]

        full = [sb("w0f", [P, 1, 4 * H0]), sb("u0f", [P, 2, 4 * H0]), sb("w1f", [P, 2, 4 * H1]),
                sb("u1f", [P, 1, 4 * H1])]
        w0, u0, w1, u1 = [sb(n, [P, 2, *f.shape[1:]], F16) for n, f in zip(("w0", "u0", "w1", "u1"), full)]
        bw = sb("bw", [3, NCOL], F16)
        biasf = sb("biasf", [1, NCOL])
        blow = sb("blow", [1, NCOL], F16)
        satrow = sb("satrow", [1, NCOL], F16)
        hist = sb("hist", [P, 3, 2, BODY, NB], F16)
        states = sb("states", [P, BODY, NB])
        tg = each(lambda n: sb(n, [P, NB]), "tg")
        fio = each(lambda n: sb(n, [P, 3, NB, 2]), "fio")
        cig = each(lambda n: sb(n, [P, 2, 1 + 2 * NB]), "cig")
        og = each(lambda n: sb(n, [P, NB]), "og")
        tc = each(lambda n: sb(n, [P, NB]), "tc")
        new = each(lambda n: sb(n, [P, NB]), "new")
        mask = sb("mask", [P, 2, BODY, NB], U16)
        pz = [[ctx.enter_context(nc.psum_tensor(f"z{c}{p}", [P, HALF, 4, NB], F32)) for p in range(2)] for c in "XYZ"]

        weights_in = sem("weights_in")
        sat_done = sem("sat_done")
        high_split = sem("high_split")
        low_split = sem("low_split")
        rows_in = sem("rows_in")
        state_zero = sem("state_zero")
        input_ready = each(sem, "input_ready")
        gates_ready = each(sem, "gates_ready")
        product_ready = each(sem, "product_ready")
        cell_ready = each(sem, "cell_ready")
        tanh_ready = each(sem, "tanh_ready")
        high_ready = each(sem, "high_ready")
        full_ready = each(sem, "full_ready")
        low_ready = each(sem, "low_ready")
        mask_ready = sem("mask_ready")
        lat_copied = sem("lat_copied")
        block = ctx.enter_context(nc.Block())

        @block.sync
        def _(sp):
            for t, w in zip(full, (W0, U0, W1, U1)):
                sp.dma_start(t[:, :, :], w.rearrange("(k p) n -> p k n", p=P)).then_inc(weights_in, 16)
            sp.dma_start(biasf[0:1, 0:4 * H0], b0.rearrange("(a n) -> a n", a=1)).then_inc(weights_in, 16)
            sp.dma_start(biasf[0:1, 4 * H0:], b1.rearrange("(a n) -> a n", a=1)).then_inc(weights_in, 16)
            sp.wait_ge(sat_done, 5)
            sp.dma_start(bw[2:3, :], satrow[:, :]).then_inc(rows_in, 16)
            sp.wait_ge(low_split, 5)
            sp.dma_start(bw[1:2, :], blow[:, :]).then_inc(rows_in, 16)

        @block.gpsimd
        def _(pool):
            pool.memset(satrow[:, :], 0.0).then_inc(sat_done, 1)
            pool.wait_ge(sat_done, 1)
            for base, n in ((0, H0), (4 * H0, H1)):
                pool.memset(satrow[:, base:base + n], -SAT).then_inc(sat_done, 1)
                pool.memset(satrow[:, base + n:base + 2 * n], SAT).then_inc(sat_done, 1)

            def copy_masks(half, t0):
                nc.gpsimd.tensor_copy(mask[:, 0, half * HALF:(half + 1) * HALF, :].rearrange("p t b -> p (t b)"),
                                      CNT[:, bass.ds((t0 + LAG) * NB, HALF * NB)]).then_inc(mask_ready, 1)
                nc.gpsimd.tensor_copy(mask[:, 1, half * HALF:(half + 1) * HALF, :].rearrange("p t b -> p (t b)"),
                                      CNT[:, bass.ds(t0 * NB, HALF * NB)]).then_inc(mask_ready, 1)

            def copy_out(half, at):
                nc.gpsimd.tensor_copy(LAT[:, bass.ds(at * NB, HALF * NB)],
                                      states[:, half * HALF:(half + 1) * HALF, :].rearrange("p t b -> p (t b)"))\
                    .then_inc(lat_copied, 1)

            pool.sem_inc(lat_copied, 1)
            pool.memset(LAT[:, (NBODY * BODY + HALF) * NB:], 0.0)
            copy_masks(0, 0)
            with pool.Fori(0, NBODY) as i:
                s0 = i * BODY
                pool.wait_ge(low_ready[Z], s0 + 1)
                copy_masks(1, s0 + HALF)
                pool.wait_ge(low_ready[Z], s0 + 2)
                copy_out(1, s0)
                pool.wait_ge(low_ready[Z], s0 + HALF + 1)
                copy_masks(0, s0 + BODY)
                pool.wait_ge(low_ready[Z], s0 + HALF + 2)
                copy_out(0, s0 + HALF)
            pool.wait_ge(low_ready[Z], NBODY * BODY + 1)
            copy_out(1, NBODY * BODY)

        def product(pe, out, weights, moving, start=False, stop=False):
            return pe.matmul(out, weights, moving, start=start, stop=stop, skip_group_check=True)

        TERMS = ((0, 0), (1, 0), (0, 1))

        def projections(pe, half, t0):
            n = HALF * NB
            work = []

            def add(c, g, weights, moving):
                first = not any(w[0] == c for w in work)
                work.append((c, lambda: product(pe, pz[c][half][:, :, g, :], weights, moving, start=first)))

            for c in CHAINS:
                base, size = (0, H0) if c < Z else (4 * H0, H1)
                for g, gate in enumerate(GATES):
                    col = gate * size + c % Z * P
                    add(c, g, bw[:, base + col:base + col + P], RHS[:, bass.ds((t0 + LAG * (c < Z)) * NB, n)])
                    for wp, mp in TERMS:
                        if c < Z:
                            add(c, g, w0[:, wp, 0, col:col + P], XN[:, mp, bass.ds(t0 * NB, n)])
                        else:
                            for k in range(2):
                                add(c, g, w1[:, wp, k, col:col + P],
                                    hist[:, k, mp, half * HALF:(half + 1) * HALF, :].rearrange("p t b -> p (t b)"))
            return [w[1] for w in work]

        @block.tensor
        def _(pe):
            pe.wait_ge(low_split, 5)
            pe.wait_ge(rows_in, 32)
            pe.wait_ge(state_zero, 1)
            for mm in projections(pe, 0, 0):
                mm()

            def step(j, s, project):
                half, jj = j // HALF, j % HALF
                old = (j - 2) % BODY

                def by(c, k, part, gates=range(4)):
                    for g in gates:
                        u, kk, col = (u1, 0, GATES[g] * H1) if c == Z else (u0, k, GATES[g] * H0 + c * P)
                        for wp in range(2 - part):
                            mm = product(pe, pz[c][half][:, jj, g, :], u[:, wp, kk, col:col + P],
                                         hist[:, k, part, old, :], stop=(part == 1 and k != X))
                    return mm

                HI, LO, FI, OG = 0, 1, (0, 1), (2, 3)
                pe.wait_ge(high_ready[X], s + 1)
                by(X, X, HI)
                by(Y, X, HI)
                pe.wait_ge(low_ready[X], s + 1)
                by(X, X, LO)
                pe.wait_ge(high_ready[Y], s + 1)
                by(X, Y, HI)
                pe.wait_ge(low_ready[Y], s + 1)
                by(X, Y, LO).then_inc(input_ready[X], 1)
                by(Y, X, LO)
                by(Y, Y, HI)
                by(Y, Y, LO).then_inc(input_ready[Y], 1)
                project()
                pe.wait_ge(high_ready[Z], s + 1)
                by(Z, Z, HI)
                pe.wait_ge(low_ready[Z], s + 1)
                by(Z, Z, LO).then_inc(input_ready[Z], 1)
                project()

            with pe.Fori(0, NBODY) as i:
                s0 = i * BODY
                for half in range(2):
                    work = projections(pe, 1 - half, s0 + (half + 1) * HALF)
                    for jj in range(HALF):
                        def project():
                            if jj >= 1 and work:
                                work.pop(0)()

                        step(half * HALF + jj, s0 + half * HALF + jj, project)
                    assert not work

        @block.scalar
        def _(act):
            def gates(c, j, s):
                z = pz[c][j // HALF][:, j % HALF, :, :]
                act.wait_ge(input_ready[c], s + 1)
                nc.scalar.activation(fio[c][:, :, :, 1], z[:, 0:3, :], ACT.Sigmoid, scale=1 / WSCALE)
                nc.scalar.activation(tg[c][:, :], z[:, 3, :], ACT.Tanh, scale=1 / WSCALE).then_inc(gates_ready[c], 1)

            def tanh(c, j, s):
                act.wait_ge(cell_ready[c], s + 1)
                nc.scalar.activation(tc[c][:, :], cig[c][:, (j + 1) % 2, 1::2], ACT.Tanh).then_inc(tanh_ready[c], 1)

            with act.Fori(0, NBODY) as i:
                for j in range(BODY):
                    s = i * BODY + j
                    gates(X, j, s)
                    gates(Y, j, s)
                    tanh(X, j, s)
                    gates(Z, j, s)
                    tanh(Y, j, s)
                    tanh(Z, j, s)

        @block.vector
        def _(dve):
            nc.vector.memset(hist[:, :, :, :, :], 0.0)
            nc.vector.memset(states[:, :, :], 0.0)
            for c in CHAINS:
                nc.vector.memset(cig[c][:, :, :], 0.0)
                nc.vector.memset(fio[c][:, :, :, :], 0.0)
                dve.sem_inc(high_ready[c], 1)
                dve.sem_inc(low_ready[c], 1)
                ins = nc.vector.memset(og[c][:, :], 0.0)
            ins.then_inc(state_zero, 1)
            dve.wait_ge(weights_in, 16 * 6)
            pairs = [(t[:, :, :], w[:, 0, :, :], w[:, 1, :, :]) for t, w in zip(full, (w0, u0, w1, u1))]
            pairs.append((biasf[:, :], bw[0:1, :], blow[:, :]))
            for f, hi, lo in pairs:
                nc.vector.tensor_scalar(hi, f, WSCALE, None, ALU.mult).then_inc(high_split, 1)
            dve.wait_ge(high_split, 5)
            for f, hi, lo in pairs:
                nc.vector.scalar_tensor_tensor(out=lo, in0=f, scalar=WSCALE, in1=hi, op0=ALU.mult, op1=ALU.subtract)\
                    .then_inc(low_split, 1)
            dve.wait_ge(state_zero, 1)

            def product_ig(c, j, s):
                dve.wait_ge(gates_ready[c], s + 1)
                nc.vector.tensor_tensor(cig[c][:, j % 2, 2::2], fio[c][:, 1, :, 1], tg[c][:, :], ALU.mult)\
                    .then_inc(product_ready[c], 1)

            def cell(c, j, s):
                dve.wait_ge(product_ready[c], s + 1)
                nc.vector.tensor_tensor_scan(out=cig[c][:, (j + 1) % 2, 0:2 * NB],
                                             data0=fio[c][:, 0, :, :].rearrange("p b k -> p (b k)"),
                                             data1=cig[c][:, j % 2, 1:], initial=0.0, op0=ALU.mult, op1=ALU.add)\
                    .then_inc(cell_ready[c], 1)

            def keep_o(c, j):
                nc.vector.copy_predicated(og[c][:, :], mask[:, c // Z, j, :], fio[c][:, 2, :, 1])

            def high(c, j, s):
                dve.wait_ge(tanh_ready[c], s + 1)
                nc.vector.tensor_tensor(hist[:, c, 0, (j - 1) % BODY, :], og[c][:, :], tc[c][:, :], ALU.mult)\
                    .then_inc(high_ready[c], 1)

            def whole(c, j):
                to = states[:, (j - 1) % BODY, :] if c == Z else new[c][:, :]
                nc.vector.tensor_tensor(to, og[c][:, :], tc[c][:, :], ALU.mult).then_inc(full_ready[c], 1)

            def low(c, j, s):
                at = (j - 1) % BODY
                dve.wait_ge(full_ready[c], s + 1)
                nc.vector.tensor_tensor(hist[:, c, 1, at, :], states[:, at, :] if c == Z else new[c][:, :],
                                        hist[:, c, 0, at, :], ALU.subtract).then_inc(low_ready[c], 1)

            with dve.Fori(0, NBODY) as i:
                for j in range(BODY):
                    s = i * BODY + j
                    if j % HALF == 0:
                        dve.wait_ge(mask_ready, i * 4 + 2 * (j // HALF) + 2)
                    if j % HALF == 1:
                        dve.wait_ge(lat_copied, i * 2 + j // HALF + 1)
                    product_ig(X, j, s)
                    cell(X, j, s)
                    keep_o(X, j)
                    product_ig(Y, j, s)
                    keep_o(Y, j)
                    cell(Y, j, s)
                    high(X, j, s)
                    whole(X, j)
                    product_ig(Z, j, s)
                    keep_o(Z, j)
                    low(X, j, s)
                    high(Y, j, s)
                    whole(Y, j)
                    cell(Z, j, s)
                    low(Y, j, s)
                    high(Z, j, s)
                    whole(Z, j)
                    low(Z, j, s)


def mixture(nc, tokens, ident, LAT, LAT0, ln_g, ln_b, wg_group, wg_inner, W1, b1, W2, b2, gln_g, gln_b, out, T, TP):
    G, E, _, FH = W1.shape
    HC = FH // P
    NTILE = TP // BODY
    NGATE = G + 1
    NEXP = G * E
    DEPTH = 4
    ON_ACT = (1, 3, 5, 7)
    NEND = 7
    CH = 2
    NCH = 2 * NEXP // CH
    AHEAD = DEPTH - 1
    assert NTILE % 2 == 0 and NEXP % DEPTH == 0 and DEPTH == 2 * CH
    TERMS = ((0, 0), (1, 0), (0, 1))
    with ExitStack() as ctx:
        def sb(name, shape, dt=F32):
            return ctx.enter_context(nc.sbuf_tensor(name, shape, dt))

        def psum(name):
            return ctx.enter_context(nc.psum_tensor(name, [P, 512], F32))

        def sem(name):
            return ctx.enter_context(nc.semaphore(name))

        w1 = sb("w1e", [P, 2, NEXP, FH], F16)
        w2 = sb("w2e", [P, 2, NEXP, HC, P], F16)
        b1r = sb("b1r", [NEXP * HC, P])
        b1c = sb("b1c", [P, NEXP, HC])
        b2s = sb("b2s", [NEXP, G, P])
        wg = sb("wg", [P, G])
        wi = sb("wi", [P, G, E])
        vec = sb("vec", [P, 2 + 2 * G, P])
        iota = sb("iota", [P, NGATE, E])
        iotau = sb("iotau", [P, NGATE, E], U32)
        ht = sb("ht", [P, P])
        latc = sb("latc", [P, P])
        h1 = sb("h1", [P, 2, P])
        xf = sb("xf", [P, 2, P])
        both = sb("both", [P, 2, P])
        z = sb("z", [P, 2, P])
        zn = sb("zn", [P, P])
        zs = sb("zs", [P, P])
        xfT = sb("xfT", [P, P])
        zT = sb("zT", [P, P])
        zTp = sb("zTp", [P, 2, 2, P], F16)
        stats = sb("stats_e", [P, 6])
        mv = sb("mv_e", [P, 2])
        rstd = sb("rstd_e", [P, 1])
        var = sb("var", [P, 1])
        gvar = sb("gvar", [P, 1])
        nhalf = sb("nhalf", [P, 1])
        eps = sb("eps_e", [P, 1])
        pad = sb("pad", [P, 1])
        gpad = sb("gpad", [P, 1])
        lg = sb("lg", [P, NGATE, E])
        top = sb("top", [P, NGATE, 8])
        ix = sb("ix", [P, NGATE, 8], U32)
        ixf = sb("ixf", [P, NGATE, 8])
        gap = sb("gap", [P, NGATE])
        p1 = sb("p1", [P, NGATE])
        p2 = sb("p2", [P, NGATE])
        m1 = sb("m1", [P, NGATE, E])
        m2 = sb("m2", [P, NGATE, E])
        wt = sb("wt", [P, 2, NGATE, E])
        wts = sb("wts", [P, 2, NGATE, E])
        wtT = sb("wtT", [NEXP, 2, P])
        hid = sb("hid", [P, DEPTH, HC, P])
        stage = hid[:, :, :, :].rearrange("p (a n) c d -> p a (n c d)", a=2)
        hidp = sb("hidp", [P, DEPTH, 2, HC, P], F16)
        moe = sb("moe", [P, 2, P])
        gstats = sb("gstats", [P, 6])
        gmv = sb("gmv", [P, 2])
        grstd = sb("grstd", [P, 1])
        gn = sb("gn", [P, P])
        gs = sb("gs", [P, P])
        y = sb("y", [P, P])
        acc = sb("acc", [P, P])
        res = sb("res", [P, P])
        pH = [psum(f"pH{k}") for k in range(DEPTH)]
        pO = [psum("pO0"), psum("pO1")]
        pA = psum("pA")
        pB = psum("pB")

        small_in = sem("small_in")
        b2_zero = sem("b2_zero")
        chunk_in = [sem("chunk_in0"), sem("chunk_in1")]
        chunk_high = sem("chunk_high")
        chunk_low = sem("chunk_low")
        consts = sem("econsts")
        b1_turned = sem("b1_turned")
        b1_done = sem("b1_done")
        iota_done = sem("iota_done")
        tile_in = sem("etile_in")
        lat_cut = sem("lat_cut")
        lat_turned = sem("lat_turned")
        h1_done = sem("h1_done")
        stats_done = sem("estats_done")
        mv_done = sem("emv_done")
        rstd_done = sem("erstd_done")
        xf_done = sem("xf_done")
        zn_done = sem("zn_done")
        zs_done = sem("zs_done")
        z_done = sem("z_done")
        x_turned = sem("x_turned")
        xT_done = sem("xT_done")
        zlow_done = sem("zlow_done")
        logits = sem("logits")
        lg_done = sem("lg_done")
        top_done = sem("top_done")
        gap_done = sem("gap_done")
        ix_done = sem("ix_done")
        ixf_done = sem("ixf_done")
        p_done = sem("p_done")
        eq_done = sem("eq_done")
        share_done = sem("share_done")
        wt_done = sem("wt_done")
        wts_done = sem("wts_done")
        wt_turned = sem("wt_turned")
        wtT_done = sem("wtT_done")
        bias_ready = sem("bias_ready")
        moe_begun = sem("moe_begun")
        up_ready = sem("up_ready")
        hid_ready = sem("hid_ready")
        hid_high = [sem("hid_high_a"), sem("hid_high_v")]
        hid_low = sem("hid_low")
        down_ready = sem("down_ready")
        mixed = sem("mixed")
        gstats_done = sem("gstats_done")
        gmv_done = sem("gmv_done")
        var_done = sem("var_done")
        gvar_done = sem("gvar_done")
        grstd_done = sem("grstd_done")
        gn_done = sem("gn_done")
        gs_done = sem("gs_done")
        y_done = sem("y_done")
        acc_done = sem("acc_done")
        res_done = sem("res_done")
        res_out = sem("res_out")
        block = ctx.enter_context(nc.Block())
        NSMALL = 5 + 3 * G

        def there(m):
            return m + 1 + DEPTH

        def vacant(m):
            return m + 1

        def bc(v):
            return v.rearrange("(a d) -> a d", a=1).to_broadcast([P, P])

        def parts(c, part):
            n = c % (NCH // 2) * CH
            if c < NCH // 2:
                return w1[:, part, n:n + CH, :].rearrange("p n h -> p (n h)")
            return w2[:, part, n:n + CH, :, :].rearrange("p n c d -> p (n c d)")

        @block.sync
        def _(sp):
            w1_in = W1.rearrange("g e d h -> d (g e) h")
            w2_in = W2.rearrange("g e (c p) d -> p (g e) c d", p=P)
            for c in range(NCH):
                if c >= 2:
                    sp.wait_ge(chunk_low, c - 1)
                n = c % (NCH // 2) * CH
                if c < NCH // 2:
                    sp.dma_start(stage[:, c % 2, :].rearrange("p (n h) -> p n h", h=FH), w1_in[:, n:n + CH, :])\
                        .then_inc(chunk_in[c % 2], 16)
                else:
                    sp.dma_start(stage[:, c % 2, :].rearrange("p (n c d) -> p n c d", c=HC, d=P),
                                 w2_in[:, n:n + CH, :, :]).then_inc(chunk_in[c % 2], 16)
                if c == 1:
                    sp.dma_start(b1r[:, :], b1.rearrange("g e (c p) -> (g e c) p", p=P)).then_inc(small_in, 16)
                    sp.wait_ge(b2_zero, 1)
                    for g in range(G):
                        sp.dma_start(b2s[g * E:(g + 1) * E, g, :], b2[g]).then_inc(small_in, 16)
                    sp.dma_start(wg[:, :], wg_group).then_inc(small_in, 16)
                    sp.dma_start(wi[:, :, :], wg_inner.rearrange("g d e -> d g e")).then_inc(small_in, 16)
                    sp.dma_start(vec[:, 0, :], bc(ln_g)).then_inc(small_in, 16)
                    sp.dma_start(vec[:, 1, :], bc(ln_b)).then_inc(small_in, 16)
                    for g in range(G):
                        sp.dma_start(vec[:, 2 + 2 * g, :], bc(gln_g[g])).then_inc(small_in, 16)
                        sp.dma_start(vec[:, 3 + 2 * g, :], bc(gln_b[g])).then_inc(small_in, 16)
            tiles = tokens.rearrange("(n t) b d -> n (t b) d", t=BODY)

            def load(t):
                sp.wait_ge(h1_done, t + 1)
                sp.dma_start(ht[:, :], tiles[bass.ds(t, 1)].rearrange("n p d -> (n p) d")).then_inc(tile_in, 16)

            def store(i, n):
                sp.wait_ge(res_done, i + 2)
                for b in range(NB):
                    sp.dma_start(out[b, bass.ds(i * BODY, n), :], res[b:n * NB:NB, :]).then_inc(res_out, 16)

            load(0)
            load(1)
            with sp.Fori(0, NTILE - 1) as i:
                load(i + 2)
                store(i, BODY)
            store(NTILE - 1, T - (NTILE - 1) * BODY)
            sp.wait_ge(res_out, 16 * NB * (NTILE + 2))

        @block.gpsimd
        def _(pool):
            pool.memset(b2s[:, :, :], 0.0).then_inc(b2_zero, 1)
            pool.iota(iotau[:, :, :], pattern=[[0, NGATE], [1, E]], base=0, channel_multiplier=0).then_inc(consts, 1)
            pool.memset(lg[:, 0, :], -3e38).then_inc(consts, 1)
            pool.memset(nhalf[:, :], -0.5).then_inc(consts, 1)
            pool.memset(eps[:, :], EPS).then_inc(consts, 1)
            pool.wait_ge(consts, 4)

            def root(n):
                pool.wait_ge(mv_done, n + 1)
                nc.gpsimd.tensor_tensor(var[:, :], mv[:, 1:2], eps[:, :], ALU.add).then_inc(var_done, 1)
                pool.wait_ge(var_done, n + 1)
                nc.gpsimd.tensor_tensor(rstd[:, :], var[:, :], nhalf[:, :], ALU.pow).then_inc(rstd_done, 1)

            def end(n):
                pool.wait_ge(gmv_done, n + 1)
                nc.gpsimd.tensor_tensor(gvar[:, :], gmv[:, 1:2], eps[:, :], ALU.add).then_inc(gvar_done, 1)
                pool.wait_ge(gvar_done, n + 1)
                nc.gpsimd.tensor_tensor(grstd[:, :], gvar[:, :], nhalf[:, :], ALU.pow).then_inc(grstd_done, 1)

            root(0)
            root(1)
            with pool.Fori(0, NTILE) as i:
                end(i * G)
                root(i * 2 + 2)
                root(i * 2 + 3)
                for g in range(1, G):
                    end(i * G + g)
            end(NTILE * G)

        @block.tensor
        def _(pe):
            pe.wait_ge(small_in, 16 * NSMALL)
            pe.matmul(pA[:, 0:P], b1r[:, :], ident[:, :], start=True, stop=True).then_inc(b1_turned, 1)
            pe.wait_ge(b1_done, 1)

            def head(n, t, u, in_loop=True):
                if n == 1:
                    pe.wait_ge(lat_cut, t + 1)
                    pe.transpose(pA[:, 0:P], latc[:, :], ident[:, :]).then_inc(lat_turned, 1)
                if n == 18:
                    if in_loop:
                        pe.wait_ge(moe_begun, (t - 1) * G + 18 // E + 2)
                    pe.wait_ge(z_done, t + 1)
                    pe.transpose(pA[:, 0:P], xf[:, u, :], ident[:, :])
                    pe.transpose(pB[:, 0:P], z[:, u, :], ident[:, :]).then_inc(x_turned, 1)
                if n == 21:
                    pe.wait_ge(xT_done, t + 1)
                    pe.matmul(pA[:, 0:G], xfT[:, :], wg[:, :], start=True, stop=True)
                    pe.matmul(pA[:, E:E + G * E], zT[:, :], wi[:, :, :].rearrange("p g e -> p (g e)"), start=True,
                              stop=True).then_inc(logits, 1)
                if n == 30:
                    if in_loop:
                        pe.wait_ge(moe_begun, (t - 1) * G + 30 // E + 2)
                    pe.wait_ge(wt_done, t + 1)
                    pe.matmul(pB[0:NEXP, 0:P], wt[:, u, 1:, :].rearrange("p g e -> p (g e)"), ident[:, :],
                              start=True, stop=True).then_inc(wt_turned, 1)

            def up(t, u, n):
                m = t * NEXP + n
                if n == 0:
                    pe.wait_ge(zlow_done, t + 1)
                pe.wait_ge(hid_ready, vacant(m))
                for c in range(HC):
                    for wp, zp in TERMS:
                        mm = pe.matmul(pH[n % DEPTH][:, c * P:(c + 1) * P], w1[:, wp, n, c * P:(c + 1) * P],
                                       zTp[:, u, zp, :], start=(wp + zp == 0), stop=(zp == 1))
                mm.then_inc(up_ready, 1)

            def down(t, n):
                m = t * NEXP + n
                pe.wait_ge(mixed, freed(m))
                pe.wait_ge(hid_low, there(m))
                for c in range(HC):
                    for wp, hp in TERMS:
                        mm = pe.matmul(pO[n % 2][:, 0:P], hidp[:, n % DEPTH, hp, c, :], w2[:, wp, n, c, :],
                                       start=(c + wp + hp == 0), stop=(c == HC - 1 and hp == 1))
                mm.then_inc(down_ready, 1)

            for n in range(NEXP):
                head(n, 0, 0, in_loop=False)
            pe.wait_ge(chunk_low, NCH)
            for n in range(AHEAD):
                up(0, 0, n)
            with pe.Fori(0, NTILE // 2) as pair:
                for u in range(2):
                    i = 2 * pair + u
                    for n in range(NEXP):
                        head(n, i + 1, 1 - u)
                        if n + AHEAD < NEXP:
                            up(i, u, n + AHEAD)
                        else:
                            up(i + 1, 1 - u, n + AHEAD - NEXP)
                        if n == 0:
                            pe.wait_ge(wtT_done, i + 1)
                        if n % E == 0:
                            pe.wait_ge(moe_begun, i * G + n // E + 1)
                            pe.matmul(pB[:, 0:P], wtT[:, u, :], b2s[:, n // E, :], start=True, stop=True)\
                                .then_inc(bias_ready, 1)
                        down(i, n)

        @block.scalar
        def _(act):
            for c in range(NCH):
                act.wait_ge(chunk_in[c % 2], 16 * (c // 2 + 1))
                nc.scalar.activation(parts(c, 0), stage[:, c % 2, :], ACT.Copy, scale=FSCALE).then_inc(chunk_high, 1)
            act.wait_ge(b1_turned, 1)
            nc.scalar.activation(b1c[:, :, :].rearrange("p n c -> p (n c)"), pA[:, 0:P], ACT.Copy, scale=FSCALE)\
                .then_inc(b1_done, 1)
            act.wait_ge(consts, 4)

            def head(n, t, u):
                if n == 0:
                    nc.scalar.copy(latc[:, :], LAT[:, bass.ds((t * BODY + LAT0) * NB, NT)]).then_inc(lat_cut, 1)
                if n == 19:
                    act.wait_ge(x_turned, t + 1)
                    nc.scalar.copy(xfT[:, :], pA[:, 0:P])
                    nc.scalar.copy(zT[:, :], pB[:, 0:P])
                    nc.scalar.copy(zTp[:, u, 0, :], pB[:, 0:P]).then_inc(xT_done, 1)
                if n == 25:
                    act.wait_ge(gap_done, t + 1)
                    nc.scalar.activation(p1[:, :], gap[:, :], ACT.Sigmoid)
                    nc.scalar.activation(p2[:, :], gap[:, :], ACT.Sigmoid, scale=-1.0).then_inc(p_done, 1)
                if n == 31:
                    act.wait_ge(wt_turned, t + 1)
                    nc.scalar.copy(wtT[:, u, :], pB[0:NEXP, 0:P]).then_inc(wtT_done, 1)

            def hidden(t, n):
                m = t * NEXP + n
                act.wait_ge(hid_low, vacant(m))
                act.wait_ge(up_ready, m + 1)
                for c in range(HC):
                    ins = nc.scalar.activation(hid[:, n % DEPTH, c, :], pH[n % DEPTH][:, c * P:(c + 1) * P], ACT.Relu,
                                               bias=b1c[:, n, c:c + 1])
                ins.then_inc(hid_ready, 1)
                if n % 8 in ON_ACT:
                    act.wait_ge(hid_ready, there(m))
                    nc.scalar.copy(hidp[:, n % DEPTH, 0, :, :], hid[:, n % DEPTH, :, :]).then_inc(hid_high[0], 1)

            for n in range(NEXP):
                head(n, 0, 0)
            for n in range(AHEAD):
                hidden(0, n)
            with act.Fori(0, NTILE // 2) as pair:
                for u in range(2):
                    i = 2 * pair + u
                    for n in range(NEXP):
                        head(n, i + 1, 1 - u)
                        if n + AHEAD < NEXP:
                            hidden(i, n + AHEAD)
                        else:
                            hidden(i + 1, n + AHEAD - NEXP)

        @block.vector
        def _(dve):
            dve.sem_inc(h1_done, 1)
            dve.sem_inc(hid_ready, DEPTH)
            dve.sem_inc(hid_low, DEPTH)
            dve.sem_inc(mixed, TOKENS)
            dve.sem_inc(moe_begun, 1)
            dve.sem_inc(acc_done, 1)
            dve.sem_inc(res_out, TOKENS * 16 * NB)
            nc.vector.memset(moe[:, 1, :], 0.0)
            nc.vector.memset(wt[:, 1, :, :], 0.0)
            nc.vector.memset(both[:, 1, :], 0.0)
            nc.vector.memset(acc[:, :], 0.0)
            for c in range(NCH):
                dve.wait_ge(chunk_high, c + 1)
                nc.vector.scalar_tensor_tensor(out=parts(c, 1), in0=stage[:, c % 2, :], scalar=FSCALE,
                                               in1=parts(c, 0), op0=ALU.mult, op1=ALU.subtract).then_inc(chunk_low, 1)
            dve.wait_ge(consts, 4)
            nc.vector.tensor_copy(iota[:, :, :], iotau[:, :, :]).then_inc(iota_done, 1)
            dve.wait_ge(iota_done, 1)
            dve.wait_ge(small_in, 16 * NSMALL)

            def wide(a):
                return a.rearrange("p (g a) -> p g a", a=1).to_broadcast([P, NGATE, E])

            def norm(n, k, to, src):
                if k == 0:
                    return nc.vector.bn_stats(stats[:, :], src).then_inc(stats_done, 1)
                if k == 1:
                    dve.wait_ge(stats_done, n + 1)
                    nc.vector.memset(pad[:, :], 0.0)
                    return nc.vector.bn_aggr(mv[:, :], stats[:, :]).then_inc(mv_done, 1)
                dve.wait_ge(rstd_done, n + 1)
                return nc.vector.tensor_scalar(to, src, mv[:, 0:1], rstd[:, :], ALU.subtract, ALU.mult)

            def head(n, t, u):
                if n == 2:
                    dve.wait_ge(tile_in, 16 * t + 16)
                    dve.wait_ge(lat_turned, t + 1)
                    nc.vector.tensor_tensor(h1[:, u, :], ht[:, :], pA[:, 0:P], ALU.add).then_inc(h1_done, 1)
                if n == 3:
                    dve.wait_ge(h1_done, t + 2)
                    norm(t * 2, 0, None, h1[:, u, :])
                if n == 4:
                    norm(t * 2, 1, None, None)
                if n == 7:
                    norm(t * 2, 2, xf[:, u, :], h1[:, u, :]).then_inc(xf_done, 1)
                if n == 8:
                    dve.wait_ge(xf_done, t + 1)
                    norm(t * 2 + 1, 0, None, xf[:, u, :])
                if n == 9:
                    norm(t * 2 + 1, 1, None, None)
                if n == 12:
                    norm(t * 2 + 1, 2, zn[:, :], xf[:, u, :]).then_inc(zn_done, 1)
                if n == 13:
                    dve.wait_ge(zn_done, t + 1)
                    nc.vector.tensor_tensor(zs[:, :], zn[:, :], vec[:, 0, :], ALU.mult).then_inc(zs_done, 1)
                if n == 14:
                    dve.wait_ge(zs_done, t + 1)
                    nc.vector.tensor_tensor(z[:, u, :], zs[:, :], vec[:, 1, :], ALU.add).then_inc(z_done, 1)
                if n == 15:
                    nc.vector.tensor_tensor(both[:, u, :], xf[:, u, :], h1[:, u, :], ALU.add)
                if n == 20:
                    dve.wait_ge(xT_done, t + 1)
                    nc.vector.tensor_tensor(zTp[:, u, 1, :], zT[:, :], zTp[:, u, 0, :], ALU.subtract)\
                        .then_inc(zlow_done, 1)
                if n == 22:
                    dve.wait_ge(logits, t + 1)
                    nc.vector.tensor_copy(lg[:, 0, 0:G], pA[:, 0:G])
                    nc.vector.tensor_copy(lg[:, 1:, :].rearrange("p g e -> p (g e)"), pA[:, E:E + G * E])\
                        .then_inc(lg_done, 1)
                if n == 23:
                    dve.wait_ge(lg_done, t + 1)
                    nc.vector.memset(gap[:, :], 0.0)
                    for g in range(NGATE):
                        ins = nc.vector.max(top[:, g, :], lg[:, g, :])
                    ins.then_inc(top_done, 1)
                if n == 24:
                    dve.wait_ge(top_done, t + 1)
                    nc.vector.tensor_tensor(gap[:, :], top[:, :, 0], top[:, :, 1], ALU.subtract).then_inc(gap_done, 1)
                    for g in range(NGATE):
                        ins = nc.vector.max_index(ix[:, g, :], top[:, g, :], lg[:, g, :])
                    ins.then_inc(ix_done, 1)
                if n == 25:
                    dve.wait_ge(ix_done, t + 1)
                    nc.vector.tensor_copy(ixf[:, :, :], ix[:, :, :]).then_inc(ixf_done, 1)
                if n == 26:
                    dve.wait_ge(ixf_done, t + 1)
                    nc.vector.tensor_tensor(m1[:, :, :], iota[:, :, :], wide(ixf[:, :, 0]), ALU.is_equal)
                    nc.vector.tensor_tensor(m2[:, :, :], iota[:, :, :], wide(ixf[:, :, 1]), ALU.is_equal)\
                        .then_inc(eq_done, 1)
                if n == 27:
                    dve.wait_ge(p_done, t + 1)
                    dve.wait_ge(eq_done, t + 1)
                    nc.vector.tensor_tensor(m1[:, :, :], m1[:, :, :], wide(p1[:, :]), ALU.mult)
                    nc.vector.tensor_tensor(m2[:, :, :], m2[:, :, :], wide(p2[:, :]), ALU.mult).then_inc(share_done, 1)
                if n == 28:
                    dve.wait_ge(share_done, t + 1)
                    nc.vector.tensor_tensor(wt[:, u, :, :], m1[:, :, :], m2[:, :, :], ALU.add).then_inc(wt_done, 1)
                if n == 29:
                    dve.wait_ge(wt_done, t + 1)
                    nc.vector.tensor_scalar(wts[:, u, :, :], wt[:, u, :, :], 1 / (FSCALE * FSCALE), None, ALU.mult)\
                        .then_inc(wts_done, 1)

            def end(k, i, u, g):
                n = i * G + g
                if g == 0:
                    u, last = 1 - u, G - 1
                else:
                    last = g - 1
                m = moe[:, last % 2, :]
                if k == 0:
                    dve.wait_ge(mixed, done(i * NEXP + g * E - 1))
                    nc.vector.bn_stats(gstats[:, :], m).then_inc(gstats_done, 1)
                if k == 1:
                    dve.wait_ge(gstats_done, n + 1)
                    nc.vector.memset(gpad[:, :], 0.0)
                    nc.vector.bn_aggr(gmv[:, :], gstats[:, :]).then_inc(gmv_done, 1)
                if k == 2:
                    dve.wait_ge(grstd_done, n + 1)
                    nc.vector.tensor_scalar(gn[:, :], m, gmv[:, 0:1], grstd[:, :], ALU.subtract, ALU.mult)\
                        .then_inc(gn_done, 1)
                if k == 3:
                    dve.wait_ge(gn_done, n + 1)
                    nc.vector.tensor_tensor(gs[:, :], gn[:, :], vec[:, 2 + 2 * last, :], ALU.mult).then_inc(gs_done, 1)
                if k == 4:
                    dve.wait_ge(gs_done, n + 1)
                    nc.vector.tensor_tensor(y[:, :], gs[:, :], vec[:, 3 + 2 * last, :], ALU.add).then_inc(y_done, 1)
                if k == 5:
                    dve.wait_ge(y_done, n + 1)
                    dve.wait_ge(acc_done, n + 1)
                    if last == 0:
                        nc.vector.tensor_scalar(acc[:, :], y[:, :], wt[:, u, 0, last:last + 1], None, ALU.mult)\
                            .then_inc(acc_done, 1)
                    else:
                        nc.vector.scalar_tensor_tensor(out=acc[:, :], in0=y[:, :], scalar=wt[:, u, 0, last:last + 1],
                                                       in1=acc[:, :], op0=ALU.mult, op1=ALU.add).then_inc(acc_done, 1)
                if k == 6 and g == 0:
                    dve.wait_ge(acc_done, n + 2)
                    dve.wait_ge(res_out, 16 * NB * (i + 1))
                    nc.vector.tensor_tensor(res[:, :], acc[:, :], both[:, u, :], ALU.add).then_inc(res_done, 1)

            def high(t, n):
                if n % 8 not in ON_ACT:
                    dve.wait_ge(hid_ready, there(t * NEXP + n))
                    nc.vector.tensor_copy(hidp[:, n % DEPTH, 0, :, :], hid[:, n % DEPTH, :, :]).then_inc(hid_high[1], 1)

            def low(t, n):
                on_act = n % 8 in ON_ACT
                mine = [k for k in range(NEXP) if (k % 8 in ON_ACT) == on_act]
                dve.wait_ge(hid_high[0 if on_act else 1], t * len(mine) + mine.index(n) + 1)
                nc.vector.tensor_tensor(hidp[:, n % DEPTH, 1, :, :], hid[:, n % DEPTH, :, :], hidp[:, n % DEPTH, 0, :, :],
                                        ALU.subtract).then_inc(hid_low, 1)

            def mix(i, u, n):
                m = i * NEXP + n
                to = moe[:, n // E % 2, :]
                if n % E == 0:
                    dve.wait_ge(moe_begun, i * G + n // E + 2)
                dve.wait_ge(mixed, freed(m + 1))
                dve.wait_ge(down_ready, m + 1)
                nc.vector.scalar_tensor_tensor(out=to, in0=pO[n % 2][:, 0:P],
                                               scalar=wts[:, u, 1 + n // E, n % E:n % E + 1], in1=to,
                                               op0=ALU.mult, op1=ALU.add).then_inc(mixed, 1)

            for n in range(NEXP):
                head(n, 0, 0)
            for n in range(AHEAD):
                high(0, n)
                low(0, n)
            with dve.Fori(0, NTILE // 2) as pair:
                for u in range(2):
                    i = 2 * pair + u
                    for n in range(NEXP):
                        t, nn = (i, n + AHEAD) if n + AHEAD < NEXP else (i + 1, n + AHEAD - NEXP)
                        high(t, nn)
                        head(n, i + 1, 1 - u)
                        if n % E == 0:
                            g = n // E
                            dve.wait_ge(wts_done, i + 1)
                            dve.wait_ge(bias_ready, i * G + g + 1)
                            nc.vector.tensor_tensor(moe[:, g % 2, :], z[:, u, :], pB[:, 0:P], ALU.add)\
                                .then_inc(moe_begun, 1)
                        mix(i, u, n)
                        low(t, nn)
                        k = n % E
                        if k != 2:
                            end(k - (k > 2), i, u, n // E)
            for k in range(NEND):
                end(k, NTILE, 0, 0)


def fusion_kernel(nc, x, txt, tok_W, tok_b, tok_cls, W0, U0, b0, W1, U1, b1, ln_g, ln_b, wg_group, wg_inner,
                  fW1, fb1, fW2, fb2, gln_g, gln_b, out):
    T = 1 + (x.shape[2] // 4) * (x.shape[3] // 4) + txt.shape[1]
    assert x.shape[0] == NB and txt.shape[2] == P and (T + LAG) % BODY == 0
    NBODY = (T + LAG) // BODY
    TP = NBODY * BODY
    TX = TP + HALF
    LAT0 = LAG - 1 + HALF
    tokens = nc.dram_tensor("tokens", [TP + BODY, NB, P], F32, kind="Internal").ap()
    with ExitStack() as ctx:
        def sb(name, shape, dt=F32):
            return ctx.enter_context(nc.sbuf_tensor(name, shape, dt))

        ident = sb("ident", [P, P])
        LAT = sb("LAT", [P, (TP + BODY + LAT0) * NB])
        with ExitStack() as inner:
            XN = inner.enter_context(nc.sbuf_tensor("XN", [P, 2, TX * NB], F16))
            CNT = inner.enter_context(nc.sbuf_tensor("CNT", [P, (LAG + TX) * NB], U16))
            RHS = inner.enter_context(nc.sbuf_tensor("RHS", [3, (LAG + TX) * NB], F16))
            make_tokens(nc, tokens, ident, XN, CNT, RHS, x, txt, tok_W, tok_b, tok_cls, T, TP)
            recur(nc, XN, CNT, RHS, LAT, W0, U0, b0, W1, U1, b1, NBODY)
        mixture(nc, tokens, ident, LAT, LAT0, ln_g, ln_b, wg_group, wg_inner, fW1, fb1, fW2, fb2, gln_g, gln_b,
                out, T, TP)


_INS = ['x', 'txt', 'L0_tok_W', 'L0_tok_b', 'L0_tok_cls', 'L0_attn_W0', 'L0_attn_U0', 'L0_attn_b0', 'L0_attn_W1',
        'L0_attn_U1', 'L0_attn_b1', 'L0_ffn_ln_g', 'L0_ffn_ln_b', 'L0_ffn_wg_group', 'L0_ffn_wg_inner', 'L0_ffn_W1',
        'L0_ffn_b1', 'L0_ffn_W2', 'L0_ffn_b2', 'L0_ffn_gln_g', 'L0_ffn_gln_b']


def kernel(**inputs):
    import numpy as _np
    import concourse.bacc as _bacc
    from concourse import mybir as _mybir
    from concourse.bass_utils import run_bass_kernel_spmd as _run

    nc = _bacc.Bacc("TRN2", target_bir_lowering=False, num_devices=1)
    arrays, args = {}, []
    for name in _INS:
        a = _np.ascontiguousarray(inputs[name])
        arrays[f"in_{name}_dram"] = a
        args.append(nc.dram_tensor(f"in_{name}_dram", a.shape, _mybir.dt.from_np(a.dtype), kind="ExternalInput").ap())
    x, txt = inputs['x'], inputs['txt']
    shape = (x.shape[0], 1 + (x.shape[2] // 4) * (x.shape[3] // 4) + txt.shape[1], txt.shape[2])
    out = nc.dram_tensor("out_0_dram", shape, _mybir.dt.float32, kind="ExternalOutput").ap()
    fusion_kernel(nc, *args, out)
    r = _run(nc, [arrays], core_ids=[0])
    return r.results[0]["out_0_dram"]
```
